# Optimizing a Trainium2 kernel written in Bass

```python
import numpy as np
import jax
import jax.numpy as jnp

def _softmax(x, axis=-1):
    return jax.nn.softmax(x, axis=axis)

def _gelu(x):
    return jax.nn.gelu(x, approximate=True)

def _silu(x):
    return jax.nn.silu(x)

def _sigmoid(x):
    return jax.nn.sigmoid(x)

def _layernorm(x, axis=-1, eps=1e-05):
    m = jnp.mean(x, axis=axis, keepdims=True)
    v = jnp.var(x, axis=axis, keepdims=True)
    return (x - m) / jnp.sqrt(v + eps)

def _scatter_add(tgt, idx, src, axis=0):
    return tgt.at[idx].add(src)

def _segment_sum(src, seg, n):
    return jax.ops.segment_sum(src, seg, n)
kernel_name = 'mk_macaron_d1_jaxref_r8_437aff'

def setup_inputs(seed: int=0):
    np.random.seed(seed)
    _w = jnp.asarray

    def _L0_attn_setup():
        import jax, jax.numpy as jnp
        import numpy as np
        B, S, H = (1, 256, 128)
        INTER, K, DST, DTR = (256, 4, 16, 64)

        def _ssm(dA, dBu, C):
            xs = (jnp.moveaxis(dA, 1, 0), jnp.moveaxis(dBu, 1, 0), jnp.moveaxis(C, 1, 0))
            state0 = jnp.zeros(dA.shape[:1] + dA.shape[2:], dA.dtype)

            def step(state, inp):
                Ai, dBui, Ci = inp
                state = Ai * state + dBui
                y = jnp.einsum('bhd,bd->bh', state, Ci)
                return (state, y)
            _, ys = jax.lax.scan(step, state0, xs)
            return jnp.moveaxis(ys, 0, 1)
        key = jax.random.key(seed)
        ks = jax.random.split(key, 10)
        sc = 0.02
        return {'x': jax.random.normal(ks[0], (B, S, H), jnp.float32), 'W_in': jax.random.normal(ks[1], (H, 2 * INTER), jnp.float32) * sc, 'conv_w': jax.random.normal(ks[2], (K, 1, INTER), jnp.float32) * sc, 'conv_b': jax.random.normal(ks[3], (INTER,), jnp.float32) * sc, 'W_x': jax.random.normal(ks[4], (INTER, DTR + 2 * DST), jnp.float32) * sc, 'W_dt': jax.random.normal(ks[5], (DTR, INTER), jnp.float32) * sc, 'b_dt': jax.random.normal(ks[6], (INTER,), jnp.float32) * sc, 'A_log': jax.random.normal(ks[7], (INTER, DST), jnp.float32) * sc, 'D': jax.random.normal(ks[8], (INTER,), jnp.float32) * sc, 'W_out': jax.random.normal(ks[9], (INTER, H), jnp.float32) * sc}
    _L0_attn_in = _L0_attn_setup()

    def _L0_ffn_setup():
        import jax, jax.numpy as jnp
        import numpy as np
        D = 128
        H = 512
        E = 64
        K = 3
        B, S = (2, 256)
        C = 64
        key = jax.random.key(seed)
        ks = jax.random.split(key, 6)
        s = 0.02
        return {'x': jax.random.normal(ks[0], (B, S, D), jnp.float32), 'gate_w': jax.random.normal(ks[1], (D, E), jnp.float32) * s, 'gate_b': jnp.zeros((E,), jnp.float32), 'w1': jax.random.normal(ks[2], (E, D, H), jnp.float32) * s, 'b1': jnp.zeros((E, H), jnp.float32), 'w2': jax.random.normal(ks[3], (E, H, D), jnp.float32) * s, 'b2': jnp.zeros((E, D), jnp.float32)}
    _L0_ffn_in = _L0_ffn_setup()
    _d = {'L0_attn_x': _L0_attn_in['x'], 'L0_attn_W_in': _L0_attn_in['W_in'], 'L0_attn_conv_w': _L0_attn_in['conv_w'], 'L0_attn_conv_b': _L0_attn_in['conv_b'], 'L0_attn_W_x': _L0_attn_in['W_x'], 'L0_attn_W_dt': _L0_attn_in['W_dt'], 'L0_attn_b_dt': _L0_attn_in['b_dt'], 'L0_attn_A_log': _L0_attn_in['A_log'], 'L0_attn_D': _L0_attn_in['D'], 'L0_attn_W_out': _L0_attn_in['W_out'], 'L0_ffn_gate_w': _L0_ffn_in['gate_w'], 'L0_ffn_gate_b': _L0_ffn_in['gate_b'], 'L0_ffn_w1': _L0_ffn_in['w1'], 'L0_ffn_b1': _L0_ffn_in['b1'], 'L0_ffn_w2': _L0_ffn_in['w2'], 'L0_ffn_b2': _L0_ffn_in['b2']}
    _x0 = _d['L0_attn_x']
    _d['L0_attn_x'] = jax.random.normal(jax.random.fold_in(jax.random.key(seed), 1), (16, 256, 128), dtype=_x0.dtype)
    del _x0
    return _d

def reference(L0_attn_x, L0_attn_W_in, L0_attn_conv_w, L0_attn_conv_b, L0_attn_W_x, L0_attn_W_dt, L0_attn_b_dt, L0_attn_A_log, L0_attn_D, L0_attn_W_out, L0_ffn_gate_w, L0_ffn_gate_b, L0_ffn_w1, L0_ffn_b1, L0_ffn_w2, L0_ffn_b2):

    def _L0_attn_ref(x, W_in, conv_w, conv_b, W_x, W_dt, b_dt, A_log, D, W_out):
        import jax, jax.numpy as jnp
        import numpy as np
        B, S, H = (1, 256, 128)
        INTER, K, DST, DTR = (256, 4, 16, 64)

        def _ssm(dA, dBu, C):
            xs = (jnp.moveaxis(dA, 1, 0), jnp.moveaxis(dBu, 1, 0), jnp.moveaxis(C, 1, 0))
            state0 = jnp.zeros(dA.shape[:1] + dA.shape[2:], dA.dtype)

            def step(state, inp):
                Ai, dBui, Ci = inp
                state = Ai * state + dBui
                y = jnp.einsum('bhd,bd->bh', state, Ci)
                return (state, y)
            _, ys = jax.lax.scan(step, state0, xs)
            return jnp.moveaxis(ys, 0, 1)
        proj = x @ W_in
        raw, gate = jnp.split(proj, 2, axis=-1)
        conv = jax.lax.conv_general_dilated(raw, conv_w, window_strides=(1,), padding=[(K - 1, 0)], dimension_numbers=('NWC', 'WIO', 'NWC'), feature_group_count=INTER)
        h = jax.nn.silu(conv + conv_b)
        ssm_p = h @ W_x
        ts, Bmat, C = jnp.split(ssm_p, [DTR, DTR + DST], axis=-1)
        dt = jax.nn.softplus(ts @ W_dt + b_dt)
        A = -jnp.exp(A_log)
        dA = jnp.exp(dt[..., None] * A)
        dBu = dt[..., None] * Bmat[:, :, None, :] * h[..., None]
        y = _ssm(dA, dBu, C)
        y = y + h * D
        y = y * jax.nn.silu(gate)
        return y @ W_out

    def _L0_ffn_ref(x, gate_w, gate_b, w1, b1, w2, b2):
        import jax, jax.numpy as jnp
        import numpy as np
        D = 128
        H = 512
        E = 64
        K = 3
        B, S = (2, 256)
        C = 64
        xf = x.reshape(-1, D)
        T = xf.shape[0]
        logits = xf @ gate_w + gate_b
        top_l, top_i = jax.lax.top_k(logits, K)
        gates = jax.nn.softmax(top_l, axis=-1)
        fe = top_i.reshape(-1)
        fg = gates.reshape(-1)
        tok = jnp.repeat(jnp.arange(T), K)
        oh = jax.nn.one_hot(fe, E, dtype=jnp.int32)
        pos = (jnp.cumsum(oh, axis=0) * oh).sum(-1) - 1
        valid = pos < C
        buf = jnp.zeros((E, C, D), x.dtype).at[fe, pos].set(xf[tok], mode='drop')
        h = jax.nn.gelu(jnp.einsum('ecd,edh->ech', buf, w1) + b1[:, None, :], approximate=False)
        y = jnp.einsum('ech,ehd->ecd', h, w2) + b2[:, None, :]
        rows = y[fe, jnp.minimum(pos, C - 1)] * (fg * valid.astype(x.dtype))[:, None]
        out = jnp.zeros_like(xf).at[tok].add(rows)
        return out.reshape(x.shape)
    x = L0_attn_x
    x = x + 0.5 * _L0_ffn_ref(_layernorm(x, axis=-1), L0_ffn_gate_w, L0_ffn_gate_b, L0_ffn_w1, L0_ffn_b1, L0_ffn_w2, L0_ffn_b2)
    x = x + _L0_attn_ref(_layernorm(x, axis=-1), L0_attn_W_in, L0_attn_conv_w, L0_attn_conv_b, L0_attn_W_x, L0_attn_W_dt, L0_attn_b_dt, L0_attn_A_log, L0_attn_D, L0_attn_W_out)
    x = x + 0.5 * _L0_ffn_ref(_layernorm(x, axis=-1), L0_ffn_gate_w, L0_ffn_gate_b, L0_ffn_w1, L0_ffn_b1, L0_ffn_w2, L0_ffn_b2)
    return x

_drawn_inputs = setup_inputs


def setup_inputs(seed=0):
    import zlib

    import numpy as np

    out = dict(_drawn_inputs(seed))
    spreads = {'L0_ffn_gate_b': (0.0, 0.1), 'L0_ffn_b1': (0.0, 0.8), 'L0_ffn_b2': (0.0, 0.1)}
    factors = {'L0_attn_W_in': 8.0,
     'L0_attn_conv_w': 8.0,
     'L0_attn_conv_b': 8.0,
     'L0_attn_W_x': 8.0,
     'L0_attn_b_dt': 8.0,
     'L0_attn_A_log': 8.0,
     'L0_attn_D': 8.0,
     'L0_attn_W_out': 8.0,
     'L0_ffn_w1': 3.287,
     'L0_ffn_w2': 2.974}
    for name, (base, spread) in spreads.items():
        noise = np.random.default_rng([zlib.crc32(name.encode()), seed]).standard_normal(out[name].shape)
        drawn = base * np.exp(spread * noise) if base else spread * noise
        out[name] = jnp.asarray(drawn.astype(out[name].dtype))
    for name, factor in factors.items():
        out[name] = (out[name] * factor).astype(out[name].dtype)
    return out
```

```python
import concourse.bass as bass
from concourse import mybir
from contextlib import ExitStack

FP = mybir.dt.float32
BF = mybir.dt.bfloat16
I32 = mybir.dt.int32
U32 = mybir.dt.uint32
ALU = mybir.AluOpType
ACT = mybir.ActivationFunctionType

P = 128
T = 4096
D = 128
NI = T // P
E = 64
CAP = 64
H = 512
HC = H // P
K = 3
PAIRS = E // 2
RING = 8
ROUNDS = PAIRS // RING
BS, SEQ = 16, 256
C2 = 2
NS = 16
DTR = 64
KC = 4
CH = 512
NQ = T // CH
EPS = 1e-5


class Sems:

    def __init__(self, ctx, nc, prefix):
        self._c, self._nc, self._p, self._d = ctx, nc, prefix, {}

    def again(self, use, totals):
        return Use(self, use, totals)

    def __call__(self, name):
        if name not in self._d:
            self._d[name] = self._c.enter_context(self._nc.semaphore(f"{self._p}_{name}"))
        return self._d[name]


class Use:
    def __init__(self, sems, use, totals):
        self._s, self._u, self._t = sems, use, totals

    def __call__(self, name):
        return self._s(name)

    def at(self, name, value):
        return self._s(name), self._u * self._t[name] + value


LN_TOTALS = dict(stats=NI, meanvar=NI, var=1, rstd=1, normed=NI, transposed=8, xT=8)
MOE_TOTALS = dict(logits=4, L=4, m8=NI, ix8=NI, ixf=1, mdiff=1, gexp=1, gs=3, V=K * NI, codesT=4, VT=4,
                  cand=16, moved=1, merged=17, slots2_zero=1, slots2=2, slotcode=1, decode=10, xn_stored=16,
                  zeroed=16 * K, x_psum=PAIRS, xt=PAIRS, h_psum=PAIRS, hb=PAIRS, hT=PAIRS, y_psum=PAIRS,
                  yt=PAIRS, o_psum=PAIRS, yo=PAIRS, x=K * NI)


def macaron(nc, x_in, W_in, conv_w, conv_b, W_x, W_dt, b_dt, A_log, D_w, W_out,
            gate_w, gate_b, w1, b1, w2, b2, out):
    ctx = ExitStack()
    with ctx:
        def sb(name, shape, dt=FP):
            return ctx.enter_context(nc.sbuf_tensor(name, shape, dt))

        xn_dram = [nc.dram_tensor(f"xn_dram{f}", [T, D], FP).ap() for f in range(2)]
        y_dram = [nc.dram_tensor(f"y_dram{f}", [K * T, D], FP).ap() for f in range(2)]

        X = sb("X", [P, NI, D])
        R1 = sb("R1", [P, 4096])
        R2 = sb("R2", [P, 4096])
        BIG = sb("BIG", [P, 32768])
        ident = sb("ident", [P, P])
        ones = sb("ones", [1, P])
        zeros = sb("zeros", [P, 512])
        gw = sb("gw", [P, E])
        gb = sb("gb", [1, E])
        b1T = sb("b1T", [P, PAIRS * 2 * HC])
        b2T = sb("b2T", [P, PAIRS * 2])
        Win = sb("Win", [P, 2 * C2 * P])
        vrow = sb("vrow", [8, C2 * P])
        vcol = sb("vcol", [P, C2, 8])
        Wx = sb("Wx", [P, C2, DTR + 2 * NS])
        Wbc = sb("Wbc", [P, C2, P])
        Wdt = sb("Wdt", [DTR, C2 * P])
        Wout = sb("Wout", [P, C2, D])
        An = sb("An", [P, C2, NS])
        sel = sb("sel", [P, 2 * NS, P], BF)
        stack = sb("stack", [P, T], BF)
        st = sb("st", [P, NI, 6])
        mv = sb("mv", [P, NI, 2])
        rstd = sb("rstd", [P, NI])
        mhalf = sb("mhalf", [P, NI])
        gate = sb("gate", [P, NI, K])
        gsum = sb("gsum", [P, NI])
        iotaE = sb("iotaE", [P, E])
        code = sb("code", [P, NI, K])
        ixf = sb("ixf", [P, NI, K])
        cf = sb("cf", [P, PAIRS])
        ci = sb("ci", [P, PAIRS], I32)
        si = sb("si", [P, PAIRS], I32)
        sf = sb("sf", [P, PAIRS])
        rf = sb("rf", [P, 3, PAIRS])
        tok_idx = sb("tok_idx", [P, PAIRS], I32)
        row_idx = sb("row_idx", [P, PAIRS], I32)

        small = stack[:, :].bitcast(FP)
        rows = small[0:E, 0:H + D]
        m8 = small[:, 640:896].rearrange("p (i k) -> p i k", k=8)
        ix8 = small[:, 896:1152].bitcast(U32).rearrange("p (i k) -> p i k", k=8)
        cand = small[:, 1152:1280]
        slots = small[0:E, 1280:1344]
        slots2 = small[0:E, 1344:1600].rearrange("p (a n) -> p a n", a=2)

        XN = R1[:, :].rearrange("p (i d) -> p i d", d=D)
        XT = R2[:, :]
        w1s = [BIG[:, 2048 * s:2048 * s + 1024].rearrange("p (a h) -> p a h", a=2) for s in range(RING)]
        w2s = [BIG[:, 2048 * s + 1024:2048 * s + 2048].rearrange("p (a c d) -> p a c d", a=2, c=HC)
               for s in range(RING)]
        B0 = 2048 * RING
        L = BIG[:, B0:B0 + 2048].rearrange("p (i e) -> p i e", e=E)
        V = [BIG[:, B0 + 2048 * (k + 1):B0 + 2048 * (k + 2)]
             .rearrange("p (g f e) -> p g f e", f=2, e=E) for k in range(K)]
        VT = R2[:, 0:2048]
        B1 = B0 + 8192
        hb = [BIG[:, B1 + 512 * u:B1 + 512 * u + 512] for u in range(2)]
        hT = [BIG[:, B1 + 1024 + 512 * u:B1 + 1536 + 512 * u].rearrange("p (a c n) -> p a c n", a=2, c=HC)
              for u in range(2)]
        xt = [BIG[:, B1 + 2048 + 128 * u:B1 + 2176 + 128 * u] for u in range(2)]
        yt = [BIG[:, B1 + 2304 + 128 * u:B1 + 2432 + 128 * u] for u in range(2)]
        yo = [BIG[:, B1 + 2560 + 128 * s:B1 + 2688 + 128 * s] for s in range(RING)]
        assert B1 + 2560 + 128 * RING <= 32768
        xg = [R1[:, 128 * s:128 * s + 128] for s in range(RING)]
        YK = BIG[:, 0:K * 4096].rearrange("p (k i d) -> p k i d", k=K, d=D)
        DT, DTU, HH, SG = [BIG[:, 8192 * m:8192 * m + 8192].rearrange("p (h t) -> p h t", h=C2)
                           for m in range(4)]
        pad = BIG[:, 0:2 * C2 * 2 * 259].rearrange("p (u h b t) -> p u h b t", u=2, h=C2, b=2)
        cv = BIG[:, 4200:4200 + 2 * C2 * CH].rearrange("p (u h t) -> p u h t", u=2, h=C2)
        ts = R1[0:DTR, 0:2 * CH].rearrange("p (u t) -> p u t", u=2)
        bcr = R1[:, 1024:2048].rearrange("p (u t) -> p u t", u=2)
        sp = R1[:, 2048:4096].rearrange("p (u h t) -> p u h t", u=2, h=C2)
        rl = R2[:, 0:2048].rearrange("p (u h t) -> p u h t", u=2, h=C2)
        dA = R1[:, 0:2048].rearrange("p (u h b t) -> p u h b t", u=2, h=C2, b=2)
        stt = R1[:, 2048:4096].rearrange("p (u h t) -> p u h t", u=2, h=C2)
        prod = R2[:, 0:2048].rearrange("p (u h t) -> p u h t", u=2, h=C2)
        Cs = R2[:, 2048:3072].rearrange("p (u t) -> p u t", u=2)
        ytmp = R2[:, 3072:4096].rearrange("p (h t) -> p h t", h=C2)

        ps = ctx.enter_context(nc.psum_tensor("ps", [P, 8, 512], FP))

        G = Sems(ctx, nc, "g")
        M = Sems(ctx, nc, "m")
        moe_sems, ln_sems = Sems(ctx, nc, "e"), Sems(ctx, nc, "l")
        F = [moe_sems.again(n, MOE_TOTALS) for n in range(2)]
        LNS = [ln_sems.again(n, LN_TOTALS) for n in range(3)]

        w1v = w1.rearrange("(a j) d h -> j d a h", a=2)
        w2v = w2.rearrange("(a j) (p c) d -> j p a (c d)", a=2, c=HC)

        def ln_vector(e, S):
            for i in range(NI):
                nc.vector.bn_stats(st[:, i, :], X[:, i, :]).then_inc(S("stats"), 1)
            for i in range(NI):
                e.wait_ge(*S.at("stats", i + 1))
                nc.vector.bn_aggr(mv[:, i, :], st[:, i, :]).then_inc(S("meanvar"), 1)
            e.wait_ge(*S.at("rstd", 1))
            for i in range(NI):
                nc.vector.tensor_scalar(XN[:, i, :], X[:, i, :], mv[:, i, 0:1], rstd[:, i:i + 1],
                                        ALU.subtract, ALU.mult).then_inc(S("normed"), 1)

        def ln_pool(e, S):
            e.wait_ge(*S.at("meanvar", NI))
            nc.gpsimd.tensor_scalar(rstd[:, :], mv[:, :, 1], EPS, None, ALU.add).then_inc(S("var"), 1)
            e.wait_ge(*S.at("var", 1))
            nc.gpsimd.tensor_tensor(rstd[:, :], rstd[:, :], mhalf[:, :], ALU.pow).then_inc(S("rstd"), 1)

        def ln_transpose(e, S, g):
            e.wait_ge(*S.at("normed", 4 * g + 4))
            if g >= 2:
                e.wait_ge(*S.at("xT", g - 1))
            for k in range(4):
                last = nc.tensor.transpose(ps[:, g % 2, k * P:(k + 1) * P], XN[:, 4 * g + k, :], ident[:, :])
            last.then_inc(S("transposed"), 1)

        def ln_copy(e, S, g, in_time_order):
            e.wait_ge(*S.at("transposed", g + 1))
            src = ps[:, g % 2, :].rearrange("d (k p) -> d k p", k=4)
            if in_time_order:
                dst = XT.rearrange("d (p i) -> d i p", i=NI)[:, 4 * g:4 * g + 4, :]
            else:
                dst = XT.rearrange("d (i p) -> d i p", i=NI)[:, 4 * g:4 * g + 4, :]
            nc.scalar.activation(dst, src, ACT.Copy).then_inc(S("xT"), 1)

        def moe_sync(e, S, f):
            def weights(r, s):
                j = RING * r + s
                e.dma_start(w1s[s], w1v[bass.ds(j, 1)].rearrange("o d a h -> (o d) a h")).then_inc(G(f"w1_{s}"), 16)
                e.dma_start(BIG[:, 2048 * s + 1024:2048 * s + 2048].rearrange("p (a h) -> p a h", a=2),
                            w2v[bass.ds(j, 1)].rearrange("o p a h -> (o p) a h")).then_inc(G(f"w2_{s}"), 16)

            for s in range(RING):
                weights(0, s)
            if f == 0:
                for k in range(K):
                    e.dma_start(y_dram[0][k * T:(k + 1) * T, :].rearrange("(p a i) d -> p a (i d)", p=P, a=8),
                                zeros[:, :].unsqueeze(1).broadcast_to([P, 8, 512])).then_inc(S("zeroed"), 16)
            with e.Fori(1, ROUNDS) as r:
                for s in range(RING):
                    e.wait_ge(*S.at("y_psum", RING * r + s - RING + 1))
                    weights(r, s)
            e.wait_ge(*S.at("y_psum", PAIRS))
            for s in range(RING):
                e.wait_ge(G(f"scattered{s}"), 16 * ROUNDS * (f + 1))
            yv = y_dram[f].rearrange("(k p i) d -> k p i d", k=K, p=P)
            for q in range(4):
                for k in range(K):
                    e.dma_start(YK[:, k, 8 * q:8 * q + 8, :], yv[k, :, 8 * q:8 * q + 8, :])\
                        .then_inc(G(f"yk{q}"), 16)

        def moe_scalar(e, S, LS, f):
            for g in range(8):
                ln_copy(e, LS, g, False)
                if g >= 4 and g % 2 == 0:
                    logits_copy(e, S, (g - 4) // 2)
            logits_copy(e, S, 2)
            logits_copy(e, S, 3)
            for b in range(4):
                e.wait_ge(*S.at("codesT", b + 1))
                nc.scalar.activation(VT[:, 512 * b:512 * b + 512], ps[:, 4 + b, :], ACT.Copy).then_inc(S("VT"), 1)
            e.wait_ge(*S.at("mdiff", 1))
            nc.scalar.activation(gate[:, :, :], gate[:, :, :], ACT.Exp).then_inc(S("gexp"), 1)

            def xt_copy(j, s):
                e.wait_ge(*S.at("x_psum", j + 1))
                if not (type(j) is int and j < 2):
                    e.wait_ge(*S.at("h_psum", j - 1))
                nc.scalar.activation(xt[s % 2], ps[:, s % 2, 0:P], ACT.Copy).then_inc(S("xt"), 1)

            def gelu(j, s):
                e.wait_ge(*S.at("hb", j + 1))
                if not (type(j) is int and j < 2):
                    e.wait_ge(*S.at("y_psum", j - 1))
                nc.scalar.activation(hT[s % 2].rearrange("p a c n -> p (a c n)"), hb[s % 2], ACT.Gelu)\
                    .then_inc(S("hT"), 1)

            def yo_copy(j, s, r):
                e.wait_ge(*S.at("o_psum", j + 1))
                e.wait_ge(G(f"scattered{s}"), 16 * (ROUNDS * f + r))
                nc.scalar.activation(yo[s], ps[:, 6 + s % 2, 0:P], ACT.Copy).then_inc(S("yo"), 1)

            xt_copy(0, 0)
            xt_copy(1, 1)
            gelu(0, 0)
            pipeline(e, [(2, lambda j, s, r: xt_copy(j, s)), (1, lambda j, s, r: gelu(j, s)),
                         (-1, lambda j, s, r: yo_copy(j, s, r))])

        def pipeline(e, stages):
            def one(r):
                for s in range(RING):
                    for lead, do in stages:
                        j, rr = RING * r + s + lead, r
                        slot = (s + lead) % RING
                        if s + lead < 0:
                            rr = r - 1
                        elif s + lead >= RING:
                            rr = r + 1
                        if type(r) is int and not 0 <= j < PAIRS:
                            continue
                        do(j, slot, rr)
            one(0)
            with e.Fori(1, ROUNDS - 1) as r:
                one(r)
            one(ROUNDS - 1)
            for lead, do in stages:
                if lead == -1:
                    do(PAIRS - 1, RING - 1, ROUNDS - 1)

        def logits_copy(e, S, g):
            e.wait_ge(*S.at("logits", g + 1))
            nc.scalar.activation(L[:, 8 * g:8 * g + 8, :], ps[:, 2 + g % 2, :].rearrange("p (i e) -> p i e", e=E),
                                 ACT.Copy).then_inc(S("L"), 1)

        def moe_tensor(e, S, LS, f):
            def logits(g):
                e.wait_ge(*LS.at("xT", 2 * g + 2))
                if g >= 2:
                    e.wait_ge(*S.at("L", g - 1))
                for k in range(8):
                    o = ps[:, 2 + g % 2, E * k:E * k + E]
                    i = 8 * g + k
                    nc.tensor.matmul(o, XT[:, i * P:i * P + P], gw[:, :], start=True, stop=False)
                    last = nc.tensor.matmul(o, ones[0:1, :], gb[0:1, :], start=False, stop=True)
                last.then_inc(S("logits"), 1)

            for g in range(8):
                ln_transpose(e, LS, g)
                if g >= 3 and g % 2 == 1:
                    logits((g - 3) // 2)
            logits(3)
            for g in range(16):
                e.wait_ge(*S.at("V", 6 * g + 6))
                for k in range(K):
                    last = nc.tensor.matmul(ps[:, 4 + g // 4, (g % 4) * P:(g % 4 + 1) * P],
                                            V[k][:, g].rearrange("p f e -> p (f e)"), ident[:, :],
                                            start=(k == 0), stop=(k == K - 1))
                if g % 4 == 3:
                    last.then_inc(S("codesT"), 1)
            e.wait_ge(*S.at("cand", 16))
            nc.tensor.matmul(ps[0:E, 2, 0:CAP], ident[:, E:2 * E], cand[:, 0:CAP], start=True, stop=True)\
                .then_inc(S("moved"), 1)
            e.wait_ge(*S.at("slots2", 2))
            nc.tensor.matmul(ps[:, 3, 0:PAIRS], slots2[:, 0, :], ident[0:E, 0:PAIRS], start=True, stop=False)
            nc.tensor.matmul(ps[:, 3, 0:PAIRS], slots2[:, 1, :], ident[0:E, PAIRS:E], start=False, stop=True)\
                .then_inc(S("slotcode"), 1)

            def t_in(j, s, r):
                e.wait_ge(G(f"gathered{s}"), 16 * (ROUNDS * f + r + 1))
                if not (type(j) is int and j < 2):
                    e.wait_ge(*S.at("xt", j - 1))
                nc.tensor.transpose(ps[:, s % 2, 0:P], xg[s], ident[:, :]).then_inc(S("x_psum"), 1)

            def mm1(j, s, r):
                e.wait_ge(*S.at("xt", j + 1))
                e.wait_ge(G(f"w1_{s}"), 16 * (ROUNDS * f + r + 1))
                if not (type(j) is int and j < 2):
                    e.wait_ge(*S.at("hb", j - 1))
                w = w1s[s].rearrange("p a (h c) -> p a c h", c=HC)
                for a in range(2):
                    for c in range(HC):
                        o = (a * HC + c) * CAP
                        last = nc.tensor.matmul(ps[:, 2 + s % 2, o:o + CAP], w[:, a, c, :],
                                                xt[s % 2][:, a * CAP:(a + 1) * CAP], start=True, stop=True)
                last.then_inc(S("h_psum"), 1)

            def mm2(j, s, r):
                e.wait_ge(*S.at("hT", j + 1))
                e.wait_ge(G(f"w2_{s}"), 16 * (ROUNDS * f + r + 1))
                if not (type(j) is int and j < 2):
                    e.wait_ge(*S.at("yt", j - 1))
                for a in range(2):
                    for c in range(HC):
                        last = nc.tensor.matmul(ps[:, 4 + s % 2, a * CAP:(a + 1) * CAP], w2s[s][:, a, c, :],
                                                hT[s % 2][:, a, c, :], start=(c == 0), stop=(c == HC - 1))
                last.then_inc(S("y_psum"), 1)

            def t_out(j, s, r):
                e.wait_ge(*S.at("yt", j + 1))
                if not (type(j) is int and j < 2):
                    e.wait_ge(*S.at("yo", j - 1))
                nc.tensor.transpose(ps[:, 6 + s % 2, 0:P], yt[s % 2], ident[:, :]).then_inc(S("o_psum"), 1)

            t_in(0, 0, 0)
            t_in(1, 1, 0)
            mm1(0, 0, 0)
            pipeline(e, [(2, t_in), (1, mm1), (0, mm2), (-1, t_out)])

        def moe_vector(e, S, LS, f):
            ln_vector(e, LS)
            for g in range(4):
                e.wait_ge(*S.at("L", g + 1))
                for i in range(8 * g, 8 * g + 8):
                    nc.vector.max(m8[:, i, :], L[:, i, :]).then_inc(S("m8"), 1)
                for i in range(8 * g, 8 * g + 8):
                    e.wait_ge(*S.at("m8", i + 1))
                    nc.vector.max_index(ix8[:, i, :], m8[:, i, :], L[:, i, :]).then_inc(S("ix8"), 1)
            e.wait_ge(*S.at("ix8", NI))
            nc.vector.tensor_copy(ixf[:, :, :], ix8[:, :, 0:K]).then_inc(S("ixf"), 1)
            nc.vector.tensor_tensor(gate[:, :, :], m8[:, :, 0:K], m8[:, :, 0:1].broadcast_to([P, NI, K]),
                                    ALU.subtract).then_inc(S("mdiff"), 1)
            e.wait_ge(*S.at("ixf", 1))
            if f == 0:
                e.wait_ge(G("code"), 1)
            for g in range(16):
                for half in range(2):
                    i = g + 16 * half
                    for k in range(K):
                        nc.vector.tensor_scalar(V[k][:, g, half, :], iotaE[:, :], ixf[:, i, k:k + 1],
                                                code[:, i, k:k + 1], ALU.is_equal, ALU.mult)\
                            .then_inc(S("V"), 1)
            e.wait_ge(*S.at("gexp", 1))
            nc.vector.reduce_sum(gsum[:, :], gate[:, :, :], axis=mybir.AxisListType.X).then_inc(S("gs"), 1)
            e.wait_ge(*S.at("gs", 1))
            nc.vector.reciprocal(gsum[:, :], gsum[:, :]).then_inc(S("gs"), 1)
            e.wait_ge(*S.at("gs", 2))
            nc.vector.scalar_tensor_tensor(out=gate[:, :, :], in0=gate[:, :, :], scalar=0.5,
                                           in1=gsum[:, :].unsqueeze(2).broadcast_to([P, NI, K]),
                                           op0=ALU.mult, op1=ALU.mult).then_inc(S("gs"), 1)
            e.wait_ge(*S.at("VT", 4))
            for r in range(CAP // 8):
                if r:
                    e.wait_ge(*S.at("cand", 2 * r))
                c8 = cand[:, 8 * r:8 * r + 8]
                nc.vector.max(c8, VT).then_inc(S("cand"), 1)
                e.wait_ge(*S.at("cand", 2 * r + 1))
                nc.vector.match_replace(VT, c8, VT, 0.0).then_inc(S("cand"), 1)
            e.wait_ge(*S.at("moved", 1))
            nc.vector.tensor_copy(cand[0:E, CAP:2 * CAP], ps[0:E, 2, 0:CAP]).then_inc(S("merged"), 1)
            for r in range(CAP // 8):
                e.wait_ge(*S.at("merged", 2 * r + 1))
                c8 = slots[:, 8 * r:8 * r + 8]
                nc.vector.max(c8, cand[0:E, :]).then_inc(S("merged"), 1)
                e.wait_ge(*S.at("merged", 2 * r + 2))
                nc.vector.match_replace(cand[0:E, :], c8, cand[0:E, :], 0.0).then_inc(S("merged"), 1)
            nc.vector.memset(slots2[:, :, :], 0.0).then_inc(S("slots2_zero"), 1)
            e.wait_ge(*S.at("slots2_zero", 1))
            e.wait_ge(*S.at("merged", 2 * (CAP // 8) + 1))
            for a in range(2):
                nc.vector.tensor_copy(slots2[:, a, a * CAP:(a + 1) * CAP], slots[:, :]).then_inc(S("slots2"), 1)
            n = 0

            def dec(instruction):
                nonlocal n
                n += 1
                instruction.then_inc(S("decode"), 1)
                e.wait_ge(*S.at("decode", n))

            e.wait_ge(*S.at("slotcode", 1))
            dec(nc.vector.tensor_copy(cf[:, :], ps[:, 3, 0:PAIRS]))
            dec(nc.vector.tensor_scalar(ci[:, :], cf[:, :], 3.0, None, ALU.add))
            dec(nc.vector.tensor_single_scalar(si[:, :], ci[:, :], 2, ALU.arith_shift_right))
            dec(nc.vector.tensor_copy(sf[:, :], si[:, :]))
            dec(nc.vector.tensor_scalar(rf[:, 0, :], sf[:, :], -1.0, float(T), ALU.mult, ALU.add))
            dec(nc.vector.tensor_scalar(tok_idx[:, :], rf[:, 0, :], float(T - 1), None, ALU.min))
            dec(nc.vector.scalar_tensor_tensor(out=rf[:, 1, :], in0=sf[:, :], scalar=4.0, in1=cf[:, :],
                                               op0=ALU.mult, op1=ALU.subtract))
            dec(nc.vector.scalar_tensor_tensor(out=rf[:, 2, :], in0=rf[:, 1, :], scalar=float(T), in1=rf[:, 0, :],
                                               op0=ALU.mult, op1=ALU.add))
            dec(nc.vector.tensor_scalar(rf[:, 1, :], cf[:, :], 0.0, float(2 * K * T), ALU.is_equal, ALU.mult))
            dec(nc.vector.tensor_tensor(row_idx[:, :], rf[:, 2, :], rf[:, 1, :], ALU.add))

            def bias1(j, s, r):
                e.wait_ge(*S.at("h_psum", j + 1))
                if not (type(j) is int and j < 2):
                    e.wait_ge(*S.at("hT", j - 1))
                bias = b1T[:, bass.ds(2 * HC * j, 2 * HC)].unsqueeze(2).broadcast_to([P, 2 * HC, CAP])
                nc.vector.tensor_tensor(hb[s % 2].rearrange("p (c n) -> p c n", n=CAP),
                                        ps[:, 2 + s % 2, :].rearrange("p (c n) -> p c n", n=CAP), bias,
                                        ALU.add).then_inc(S("hb"), 1)

            def bias2(j, s, r):
                e.wait_ge(*S.at("y_psum", j + 1))
                if not (type(j) is int and j < 2):
                    e.wait_ge(*S.at("o_psum", j - 1))
                bias = b2T[:, bass.ds(2 * j, 2)].unsqueeze(2).broadcast_to([P, 2, CAP])
                nc.vector.tensor_tensor(yt[s % 2].rearrange("p (a n) -> p a n", n=CAP),
                                        ps[:, 4 + s % 2, 0:P].rearrange("p (a n) -> p a n", n=CAP), bias,
                                        ALU.add).then_inc(S("yt"), 1)

            bias1(0, 0, 0)
            pipeline(e, [(1, bias1), (0, bias2)])
            for q in range(4):
                e.wait_ge(G(f"yk{q}"), 16 * K * (f + 1))
                for k in range(K):
                    for i in range(8 * q, 8 * q + 8):
                        if k:
                            e.wait_ge(*S.at("x", 24 * q + 8 * (k - 1) + i - 8 * q + 1))
                        nc.vector.scalar_tensor_tensor(out=X[:, i, :], in0=YK[:, k, i, :],
                                                       scalar=gate[:, i, k:k + 1], in1=X[:, i, :],
                                                       op0=ALU.mult, op1=ALU.add).then_inc(S("x"), 1)
            e.wait_ge(*S.at("x", NI * K))

        def moe_pool(e, S, LS, f):
            ln_pool(e, LS)
            e.wait_ge(*LS.at("normed", NI))
            e.dma_start(xn_dram[f].rearrange("(p i) d -> p (i d)", p=P), R1[:, :]).then_inc(S("xn_stored"), 16)
            e.wait_ge(*S.at("xn_stored", 16))
            e.wait_ge(*S.at("decode", 10))

            def gather(j):
                s = j % RING
                if j >= RING:
                    e.wait_ge(*S.at("x_psum", j - RING + 1))
                nc.gpsimd.indirect_dma_start(
                    xg[s], None, xn_dram[f], bass.IndirectOffsetOnAxis(tok_idx[:, j:j + 1].bitcast(U32), 0),
                    bounds_check=T - 1, oob_is_err=False).then_inc(G(f"gathered{s}"), 16)

            for j in range(RING):
                gather(j)
            if f == 0:
                e.wait_ge(*S.at("zeroed", 16 * K))
            else:
                e.wait_ge(M("zeroed"), 16 * K)
            for j in range(PAIRS):
                s = j % RING
                e.wait_ge(*S.at("yo", j + 1))
                nc.gpsimd.indirect_dma_start(
                    y_dram[f], bass.IndirectOffsetOnAxis(row_idx[:, j:j + 1].bitcast(U32), 0), yo[s], None,
                    bounds_check=K * T - 1, oob_is_err=False).then_inc(G(f"scattered{s}"), 16)
                if j + RING < PAIRS:
                    gather(j + RING)

        CRED = 2

        def mamba_tensor(e):
            LS = LNS[1]
            for g in range(8):
                ln_transpose(e, LS, g)
            e.wait_ge(*LS.at("xT", 8))
            with e.Fori(0, NQ // 2) as r:
                for u in range(2):
                    q = 2 * r + u
                    rhs = XT[:, bass.ds(CH * q, CH)]
                    e.wait_ge(M("raw"), q - 2 + CRED + 1)
                    for m in range(2):
                        last = nc.tensor.matmul(ps[:, 2 * u + m, :], Win[:, m * P:(m + 1) * P], rhs,
                                                start=True, stop=True)
                    last.then_inc(M("raw_psum"), 1)
                    e.wait_ge(M("sg"), q - 2 + CRED + 1)
                    for m in range(2):
                        last = nc.tensor.matmul(ps[:, 4 + 2 * u + m, :], Win[:, (2 + m) * P:(3 + m) * P], rhs,
                                                start=True, stop=True)
                    last.then_inc(M("gate_psum"), 1)
            e.wait_ge(M("h"), NQ + CRED)
            e.wait_ge(M("sg"), NQ + CRED)
            with e.Fori(0, NQ // 2) as r:
                for u in range(2):
                    q = 2 * r + u
                    e.wait_ge(M("dt"), q - 2 + CRED + 1)
                    for h in range(C2):
                        last = nc.tensor.matmul(ps[0:DTR, 4 * u, :], Wx[:, h, 0:DTR], HH[:, h, bass.ds(CH * q, CH)],
                                                start=(h == 0), stop=(h == C2 - 1))
                    last.then_inc(M("ts_psum"), 1)
                    for h in range(C2):
                        last = nc.tensor.matmul(ps[:, 4 * u + 1, :], Wbc[:, h, :], HH[:, h, bass.ds(CH * q, CH)],
                                                start=(h == 0), stop=(h == C2 - 1))
                    last.then_inc(M("bc_psum"), 1)
                for u in range(2):
                    q = 2 * r + u
                    e.wait_ge(M("ts"), q + 1)
                    for h in range(C2):
                        last = nc.tensor.matmul(ps[:, 4 * u + 2 + h, :], Wdt[:, h * P:(h + 1) * P], ts[:, u, :],
                                                start=True, stop=True)
                    last.then_inc(M("dt_psum"), 1)
            e.wait_ge(M("dt"), NQ + CRED)
            e.wait_ge(M("stack"), NQ)

            def bcast(n, q, bank, name):
                nc.tensor.matmul(ps[:, bank, :], sel[:, n, :], stack[:, bass.ds(CH * q, CH)],
                                 start=True, stop=True).then_inc(M(name), 1)

            with e.Fori(0, NQ) as q:
                def b_and_c(n):
                    e.wait_ge(M("dbu"), 2 * (NS * q + n + CRED))
                    bcast(n, q, 2, "b_psum")
                    e.wait_ge(M("cs"), NS * q + n + CRED)
                    bcast(NS + n, q, 3, "c_psum")

                b_and_c(0)
                e.wait_ge(M("y"), 2 * q + CRED)
                for n in range(NS):
                    if n < NS - 1:
                        b_and_c(n + 1)
                    e.wait_ge(M("prod"), NS * q + n + 1 + CRED)
                    for h in range(C2):
                        last = nc.tensor.matmul(ps[:, 4 + h, :], ident[:, :], prod[:, n % 2, h, :],
                                                start=(n == 0), stop=(n == NS - 1))
                    last.then_inc(M("summed"), 1)
            e.wait_ge(M("y"), 2 * NQ + CRED)
            for g in range(8):
                if g >= 2:
                    e.wait_ge(M("x"), g - 1)
                for k in range(4):
                    for h in range(C2):
                        lhsT = SG[:, h, :].rearrange("p (q i) -> p i q", i=NI)[:, 4 * g + k, :]
                        last = nc.tensor.matmul(ps[:, g % 2, k * P:(k + 1) * P], lhsT, Wout[:, h, :],
                                                start=(h == 0), stop=(h == C2 - 1))
                last.then_inc(M("o_psum"), 1)

        def mamba_scalar(e):
            LS = LNS[1]

            def own_wait():
                e.sem_inc(M("held"), 1)

            for g in range(8):
                ln_copy(e, LS, g, True)
            with e.Fori(0, NQ // 2) as r:
                for u in range(2):
                    q = 2 * r + u
                    e.wait_ge(M("raw_psum"), q + 1)
                    e.wait_ge(M("conv"), q - 2 + CRED + 1)
                    for h in range(C2):
                        last = nc.scalar.activation(pad[:, u, h, :, 3:3 + SEQ],
                                                    ps[:, 2 * u + h, :].rearrange("p (b t) -> p b t", b=2),
                                                    ACT.Copy)
                    last.then_inc(M("raw"), 1)
                for u in range(2):
                    q = 2 * r + u
                    e.wait_ge(M("gate_psum"), q + 1)
                    own_wait()
                    nc.scalar.activation(SG[:, :, bass.ds(CH * q, CH)], ps[:, 4 + 2 * u:6 + 2 * u, :], ACT.Silu)\
                        .then_inc(M("sg"), 1)
                for u in range(2):
                    q = 2 * r + u
                    e.wait_ge(M("conv"), q + 1 + CRED)
                    own_wait()
                    nc.scalar.activation(HH[:, :, bass.ds(CH * q, CH)], cv[:, u, :, :], ACT.Silu)\
                        .then_inc(M("h"), 1)
            with e.Fori(0, NQ // 2) as r:
                for u in range(2):
                    q = 2 * r + u
                    e.wait_ge(M("ts_psum"), q + 1)
                    e.wait_ge(M("dt"), q - 2 + CRED + 1)
                    nc.scalar.activation(ts[:, u, :], ps[0:DTR, 4 * u, :], ACT.Copy).then_inc(M("ts"), 1)
                    e.wait_ge(M("bc_psum"), q + 1)
                    own_wait()
                    nc.scalar.activation(stack[:, bass.ds(CH * q, CH)], ps[:, 4 * u + 1, :], ACT.Copy)\
                        .then_inc(M("hi"), 1)
                for u in range(2):
                    q = 2 * r + u
                    e.wait_ge(M("rest"), q + 1)
                    own_wait()
                    nc.scalar.activation(stack[64:P, bass.ds(CH * q, CH)], bcr[64:P, u, :], ACT.Copy)\
                        .then_inc(M("mid"), 1)
                for u in range(2):
                    q = 2 * r + u
                    e.wait_ge(M("z"), q + 1)
                    nc.scalar.activation(sp[:, u], rl[:, u], ACT.Abs).then_inc(M("abs"), 1)
                    e.wait_ge(M("abs"), q + 1)
                    nc.scalar.activation(sp[:, u], sp[:, u], ACT.Exp, scale=-1.0).then_inc(M("exp"), 1)
                    e.wait_ge(M("exp"), q + 1)
                    nc.scalar.activation(sp[:, u], sp[:, u], ACT.Ln, bias=1.0).then_inc(M("ln"), 1)
            e.wait_ge(M("dt"), NQ + CRED)
            e.wait_ge(M("dA_zero"), 1)
            with e.Fori(0, NQ) as q:
                for n in range(NS):
                    step = NS * q + n
                    e.wait_ge(M("scanned"), 2 * (step - 2 + CRED) + 2)
                    own_wait()
                    for h in range(C2):
                        nc.scalar.activation(
                            dA[:, n % 2, h, :, 1:SEQ],
                            DT[:, h, bass.ds(CH * q, CH)].rearrange("p (b t) -> p b t", b=2)[:, :, 1:SEQ],
                            ACT.Exp, scale=An[:, h, n:n + 1]).then_inc(M("dA"), 1)
                    e.wait_ge(M("c_psum"), step + 1)
                    e.wait_ge(M("prod"), step - 2 + CRED + 1)
                    nc.scalar.activation(Cs[:, n % 2, :], ps[:, 3, :], ACT.Copy).then_inc(M("cs"), 1)

        def mamba_vector(e):
            ln_vector(e, LNS[1])
            with e.Fori(0, NQ // 2) as r:
                for u in range(2):
                    q = 2 * r + u
                    e.wait_ge(M("raw"), q + 1 + CRED)
                    e.wait_ge(M("h"), 2 * r + CRED)
                    for h in range(C2):
                        o = cv[:, u, h, :].rearrange("p (b t) -> p b t", b=2)
                        nc.vector.tensor_scalar(o, pad[:, u, h, :, 3:3 + SEQ], vcol[:, h, 3:4], vcol[:, h, 4:5],
                                                ALU.mult, ALU.add).then_inc(M("tap"), 1)
                    for k in range(KC - 1):
                        for h in range(C2):
                            o = cv[:, u, h, :].rearrange("p (b t) -> p b t", b=2)
                            e.wait_ge(M("tap"), (KC * C2) * q + C2 * k + h + 1)
                            last = nc.vector.scalar_tensor_tensor(out=o, in0=pad[:, u, h, :, k:k + SEQ],
                                                                  scalar=vcol[:, h, k:k + 1], in1=o,
                                                                  op0=ALU.mult, op1=ALU.add)
                            last.then_inc(M("tap"), 1)
                    e.wait_ge(M("tap"), KC * C2 * q + KC * C2)
                    e.sem_inc(M("conv"), 1)
            with e.Fori(0, NQ // 2) as r:
                for u in range(2):
                    q = 2 * r + u
                    e.wait_ge(M("hi"), q + 1)
                    nc.vector.tensor_tensor(bcr[:, u, :], ps[:, 4 * u + 1, :], stack[:, bass.ds(CH * q, CH)],
                                            ALU.subtract).then_inc(M("rest"), 1)
                for u in range(2):
                    q = 2 * r + u
                    e.wait_ge(M("mid"), q + 1)
                    nc.vector.tensor_tensor(stack[96:P, bass.ds(CH * q, CH)], bcr[96:P, u, :],
                                            stack[96:P, bass.ds(CH * q, CH)], ALU.subtract).then_inc(M("stack"), 1)
                for u in range(2):
                    q = 2 * r + u
                    e.wait_ge(M("dt_psum"), q + 1)
                    for h in range(C2):
                        last = nc.vector.tensor_scalar(rl[:, u, h, :], ps[:, 4 * u + 2 + h, :], vcol[:, h, 5:6], None,
                                                       ALU.add)
                    last.then_inc(M("z"), 1)
                for u in range(2):
                    q = 2 * r + u
                    e.wait_ge(M("ln"), q + 1)
                    nc.vector.scalar_tensor_tensor(out=DT[:, :, bass.ds(CH * q, CH)], in0=rl[:, u], scalar=0.0,
                                                   in1=sp[:, u], op0=ALU.max, op1=ALU.add)\
                        .then_inc(M("dt"), 1)
                    e.wait_ge(M("dt"), q + 1 + CRED)
                    nc.vector.tensor_tensor(DTU[:, :, bass.ds(CH * q, CH)], DT[:, :, bass.ds(CH * q, CH)],
                                            HH[:, :, bass.ds(CH * q, CH)], ALU.mult).then_inc(M("dtu"), 1)
            e.wait_ge(M("dtu"), NQ)
            with e.Fori(0, NQ) as q:
                for n in range(NS):
                    step = NS * q + n
                    e.wait_ge(M("b_psum"), step + 1)
                    for h in range(C2):
                        e.wait_ge(M("scanned"), 2 * (step - 1 + CRED) + h + 1)
                        nc.vector.tensor_tensor(ps[:, h, :], DTU[:, h, bass.ds(CH * q, CH)], ps[:, 2, :],
                                                ALU.mult).then_inc(M("dbu"), 1)
                    e.wait_ge(M("prod"), step - 2 + CRED + 1)
                    for h in range(C2):
                        e.wait_ge(M("dbu"), 2 * (step + CRED) + h + 1)
                        e.wait_ge(M("dA"), 2 * step + h + 1)
                        nc.vector.tensor_tensor_scan(stt[:, n % 2, h, :],
                                                     dA[:, n % 2, h, :, :].rearrange("p b t -> p (b t)"),
                                                     ps[:, h, :], 0.0, ALU.mult, ALU.add)\
                            .then_inc(M("scanned"), 1)
                e.wait_ge(M("summed"), NS * q + NS + CRED)
                for h in range(C2):
                    nc.vector.scalar_tensor_tensor(out=ytmp[:, h, :], in0=HH[:, h, bass.ds(CH * q, CH)],
                                                   scalar=vcol[:, h, 6:7], in1=ps[:, 4 + h, :],
                                                   op0=ALU.mult, op1=ALU.add).then_inc(M("y_in"), 1)
                for h in range(C2):
                    e.wait_ge(M("y_in"), 2 * q + h + 1)
                    nc.vector.tensor_tensor(SG[:, h, bass.ds(CH * q, CH)], ytmp[:, h, :],
                                            SG[:, h, bass.ds(CH * q, CH)], ALU.mult).then_inc(M("y"), 1)
            for g in range(8):
                e.wait_ge(M("o_psum"), g + 1)
                nc.vector.tensor_tensor(X[:, 4 * g:4 * g + 4, :].rearrange("p i d -> p (i d)"),
                                        X[:, 4 * g:4 * g + 4, :].rearrange("p i d -> p (i d)"), ps[:, g % 2, :],
                                        ALU.add).then_inc(M("x"), 1)
            e.wait_ge(M("x"), 8)

        def mamba_pool(e):
            ln_pool(e, LNS[1])
            e.wait_ge(M("dt"), NQ + CRED)
            nc.gpsimd.memset(dA[:, :, :, :, 0:1], 0.0).then_inc(M("dA_zero"), 1)
            with e.Fori(0, NQ) as q:
                for n in range(NS):
                    step = NS * q + n
                    e.wait_ge(M("scanned"), 2 * (step + CRED) + 2)
                    e.wait_ge(M("cs"), step + CRED + 1)
                    e.wait_ge(M("summed"), step - 2 + CRED + 1)
                    nc.gpsimd.tensor_tensor(prod[:, n % 2], stt[:, n % 2],
                                            Cs[:, n % 2, :].unsqueeze(1).broadcast_to([P, C2, CH]),
                                            ALU.mult).then_inc(M("prod"), 1)

        block = ctx.enter_context(nc.Block())

        @block.sync
        def _(e):
            e.dma_start(X[:, :, :], x_in.rearrange("b (c i) d -> (b c) i d", i=NI)).then_inc(G("x"), 16)
            e.dma_start(gw[:, :], gate_w).then_inc(G("gw"), 16)
            e.dma_start(gb[:, :], gate_b.rearrange("(a n) -> a n", a=1)).then_inc(G("gw"), 16)
            e.dma_start(rows[:, 0:H], b1).then_inc(G("rows"), 16)
            e.dma_start(rows[:, H:H + D], b2).then_inc(G("rows"), 16)
            e.wait_ge(G("zeros"), 1)
            moe_sync(e, F[0], 0)
            e.dma_start(Win[:, :], W_in).then_inc(G("mw"), 16)
            e.dma_start(Wx[:, :, :], W_x.rearrange("(h p) n -> p h n", p=P)).then_inc(G("mw"), 16)
            e.dma_start(Wdt[:, :], W_dt).then_inc(G("mw"), 16)
            e.dma_start(Wout[:, :, :], W_out.rearrange("(h p) n -> p h n", p=P)).then_inc(G("mw"), 16)
            e.dma_start(An[:, :, :], A_log.rearrange("(h p) n -> p h n", p=P)).then_inc(G("mw"), 16)
            e.dma_start(vrow[0:KC, :], conv_w.rearrange("k o c -> k (o c)")).then_inc(G("mw"), 16)
            for k, v in enumerate((conv_b, b_dt, D_w)):
                e.dma_start(vrow[KC + k:KC + k + 1, :], v.rearrange("(a c) -> a c", a=1)).then_inc(G("mw"), 16)
            for k in range(K):
                e.dma_start(y_dram[1][k * T:(k + 1) * T, :].rearrange("(p a i) d -> p a (i d)", p=P, a=8),
                            zeros[:, :].unsqueeze(1).broadcast_to([P, 8, 512])).then_inc(M("zeroed"), 16)
            e.wait_ge(M("o_psum"), 8)
            moe_sync(e, F[1], 1)
            for q in range(4):
                e.wait_ge(*F[1].at("x", 24 * q + 24))
                e.dma_start(out.rearrange("b (c i) d -> (b c) i d", i=NI)[:, 8 * q:8 * q + 8, :],
                            X[:, 8 * q:8 * q + 8, :]).then_inc(G("out"), 16)
            e.wait_ge(G("out"), 64)

        @block.gpsimd
        def _(e):
            nc.gpsimd.memset(ident[:, :], 0.0).then_inc(G("id0"), 1)
            nc.gpsimd.memset(zeros[:, :], 0.0).then_inc(G("zeros"), 1)
            nc.gpsimd.memset(ones[:, :], 1.0).then_inc(G("ones"), 1)
            nc.gpsimd.memset(mhalf[:, :], -0.5).then_inc(G("mhalf"), 1)
            e.wait_ge(G("mhalf"), 1)
            e.wait_ge(G("id0"), 1)
            nc.gpsimd.affine_select(out=ident[:, :], in_=ident[:, :], compare_op=ALU.not_equal, fill=1.0, base=0,
                                    pattern=[[-1, P]], channel_multiplier=1).then_inc(G("ident"), 1)
            nc.gpsimd.iota(iotaE[:, :], pattern=[[1, E]], base=0, channel_multiplier=0,
                           allow_small_or_imprecise_dtypes=True).then_inc(G("code"), 1)
            nc.gpsimd.iota(code[:, :, :], pattern=[[-4, NI], [-1, K]], base=4 * T, channel_multiplier=-4 * NI,
                           allow_small_or_imprecise_dtypes=True).then_inc(G("code"), 1)
            nc.gpsimd.memset(sel[:, :, :], 0.0).then_inc(G("sel0"), 1)
            nc.gpsimd.memset(vrow[:, :], 0.0).then_inc(G("vrow0"), 1)
            for name, c in (("raw", CRED), ("sg", CRED), ("conv", CRED), ("dt", CRED), ("prod", CRED),
                            ("scanned", 2 * CRED), ("summed", CRED),
                            ("h", CRED), ("dbu", 2 * CRED), ("cs", CRED), ("y", CRED)):
                e.sem_inc(M(name), c)
            e.wait_ge(G("sel0"), 1)
            for n, g in enumerate((0, 2, 3)):
                e.wait_ge(G("sel"), n)
                part = sel[32 * g:32 * g + 32, :, :]
                nc.gpsimd.affine_select(out=part, in_=part, compare_op=ALU.not_equal, fill=1.0, base=0,
                                        pattern=[[-1, 2 * NS], [0, P]], channel_multiplier=1)\
                    .then_inc(G("sel"), 1)
            e.wait_ge(G("sel"), 3)
            moe_pool(e, F[0], LNS[0], 0)
            mamba_pool(e)
            moe_pool(e, F[1], LNS[2], 1)
            for s in range(RING):
                e.wait_ge(G(f"scattered{s}"), 2 * 16 * ROUNDS)

        @block.scalar
        def _(e):
            for c in range(HC):
                e.wait_ge(G("biasT"), c + 1)
                nc.scalar.activation(b1T[:, :].rearrange("p (j a c) -> p a j c", a=2, c=HC)[:, :, :, c],
                                     ps[:, 4 + c, 0:E].rearrange("p (a j) -> p a j", a=2), ACT.Copy)\
                    .then_inc(G("bias"), 1)
            e.wait_ge(G("biasT"), HC + 1)
            nc.scalar.activation(b2T[:, :].rearrange("p (j a) -> p a j", a=2),
                                 ps[:, 3, 0:E].rearrange("p (a j) -> p a j", a=2), ACT.Copy).then_inc(G("bias"), 1)
            moe_scalar(e, F[0], LNS[0], 0)
            e.wait_ge(G("mw"), 16 * 9)
            for h in range(C2):
                e.wait_ge(G("vT"), h + 1)
                nc.scalar.activation(vcol[:, h, :], ps[:, 4 + h, 0:8], ACT.Copy).then_inc(G("vcol"), 1)
            for k in range(4):
                nc.scalar.activation(Wbc[:, :, 32 * k:32 * k + 32], Wx[:, :, DTR:DTR + 2 * NS], ACT.Copy)\
                    .then_inc(G("vcol"), 1)
            nc.scalar.activation(An[:, :, :], An[:, :, :], ACT.Exp).then_inc(G("A"), 1)
            e.wait_ge(G("A"), 1)
            nc.scalar.activation(An[:, :, :], An[:, :, :], ACT.Copy, scale=-1.0).then_inc(G("A"), 1)
            mamba_scalar(e)
            e.wait_ge(G("A"), 2)
            moe_scalar(e, F[1], LNS[2], 1)

        @block.vector
        def _(e):
            e.wait_ge(G("x"), 16)
            moe_vector(e, F[0], LNS[0], 0)
            e.wait_ge(*F[0].at("hb", PAIRS))
            nc.vector.memset(pad[:, :, :, :, 0:3], 0.0).then_inc(M("pad"), 1)
            e.wait_ge(M("pad"), 1)
            e.wait_ge(G("vcol"), C2)
            mamba_vector(e)
            moe_vector(e, F[1], LNS[2], 1)

        @block.tensor
        def _(e):
            e.wait_ge(G("ident"), 1)
            e.wait_ge(G("rows"), 32)
            for c in range(HC):
                nc.tensor.transpose(ps[:, 4 + c, 0:E], rows[:, 0:H].rearrange("e (p c) -> e c p", c=HC)[:, c, :],
                                    ident[0:E, 0:E]).then_inc(G("biasT"), 1)
            nc.tensor.transpose(ps[:, 3, 0:E], rows[:, H:H + D], ident[0:E, 0:E]).then_inc(G("biasT"), 1)
            e.wait_ge(G("bias"), HC + 1)
            e.wait_ge(G("gw"), 32)
            e.wait_ge(G("ones"), 1)
            moe_tensor(e, F[0], LNS[0], 0)
            e.wait_ge(G("mw"), 16 * 9)
            e.wait_ge(*F[0].at("yt", PAIRS))
            for h in range(C2):
                nc.tensor.transpose(ps[:, 4 + h, 0:8], vrow[:, h * P:(h + 1) * P], ident[0:8, 0:8])\
                    .then_inc(G("vT"), 1)
            e.wait_ge(G("vcol"), C2 + 4)
            e.wait_ge(G("sel"), 3)
            mamba_tensor(e)
            moe_tensor(e, F[1], LNS[2], 1)


_INS = ['L0_attn_x', 'L0_attn_W_in', 'L0_attn_conv_w', 'L0_attn_conv_b', 'L0_attn_W_x', 'L0_attn_W_dt',
        'L0_attn_b_dt', 'L0_attn_A_log', 'L0_attn_D', 'L0_attn_W_out', 'L0_ffn_gate_w', 'L0_ffn_gate_b',
        'L0_ffn_w1', 'L0_ffn_b1', 'L0_ffn_w2', 'L0_ffn_b2']
_OUTS = [((BS, SEQ, D), 'float32')]


def kernel(**inputs):
    import numpy as _np
    import concourse.bacc as _bacc
    from concourse.bass_utils import run_bass_kernel_spmd as _run

    nc = _bacc.Bacc("TRN2", target_bir_lowering=False, num_devices=1)
    arrays, args = {}, []
    for name in _INS:
        a = _np.ascontiguousarray(inputs[name])
        arrays[f"in_{name}"] = a
        args.append(nc.dram_tensor(f"in_{name}", a.shape, mybir.dt.from_np(a.dtype), kind="ExternalInput").ap())
    for i, (shape, dtype) in enumerate(_OUTS):
        dt = mybir.dt.from_np(_np.dtype(dtype))
        args.append(nc.dram_tensor(f"out_{i}", shape, dt, kind="ExternalOutput").ap())
    macaron(nc, *args)
    r = _run(nc, [arrays], core_ids=[0])
    return r.results[0]["out_0"]
```

```python
import concourse.bass as bass
from concourse import mybir
from contextlib import ExitStack

FP = mybir.dt.float32
BF = mybir.dt.bfloat16
I32 = mybir.dt.int32
U32 = mybir.dt.uint32
ALU = mybir.AluOpType
ACT = mybir.ActivationFunctionType

P = 128
T = 4096
D = 128
NI = T // P
E = 64
CAP = 64
H = 512
HC = H // P
K = 3
PAIRS = E // 2
RING = 8
ROUNDS = PAIRS // RING
BS, SEQ = 16, 256
C2 = 2
NS = 16
DTR = 64
KC = 4
CH = 512
NQ = T // CH
EPS = 1e-5


class Sems:

    def __init__(self, ctx, nc, prefix):
        self._c, self._nc, self._p, self._d = ctx, nc, prefix, {}

    def again(self, use, totals):
        return Use(self, use, totals)

    def __call__(self, name):
        if name not in self._d:
            self._d[name] = self._c.enter_context(self._nc.semaphore(f"{self._p}_{name}"))
        return self._d[name]


class Use:
    def __init__(self, sems, use, totals):
        self._s, self._u, self._t = sems, use, totals

    def __call__(self, name):
        return self._s(name)

    def at(self, name, value):
        return self._s(name), self._u * self._t[name] + value


LN_TOTALS = dict(stats=NI, meanvar=NI, rstd=16, normed=24, normed_act=8, transposed=8, xT=8)
MOE_TOTALS = dict(logits=4, L=4, m8=NI, ix8=NI, ixf=1, mdiff=1, gexp=1, gs=3, V=2 * K, codesT=4, VT=4,
                  cand=16, moved=1, merged=17, slots2_zero=1, slots2=2, slotcode=1, decode=10, xn_stored=16,
                  zeroed=16 * K, x_psum=PAIRS, xt=PAIRS, h_psum=PAIRS, hs=PAIRS, ht_psum=PAIRS, hb=PAIRS,
                  hT=PAIRS, y_psum=PAIRS, yo=PAIRS, x=K * NI)


def macaron(nc, x_in, W_in, conv_w, conv_b, W_x, W_dt, b_dt, A_log, D_w, W_out,
            gate_w, gate_b, w1, b1, w2, b2, out):
    ctx = ExitStack()
    with ctx:
        def sb(name, shape, dt=FP):
            return ctx.enter_context(nc.sbuf_tensor(name, shape, dt))

        xn_dram = [nc.dram_tensor(f"xn_dram{f}", [T, D], FP).ap() for f in range(2)]
        y_dram = [nc.dram_tensor(f"y_dram{f}", [K * T, D], FP).ap() for f in range(2)]

        X = sb("X", [P, NI, D])
        R1 = sb("R1", [P, 4096])
        R2 = sb("R2", [P, 4096])
        BIG = sb("BIG", [P, 32768])
        ident = sb("ident", [P, P])
        zeros = sb("zeros", [P, 512])
        gw = sb("gw", [P, E])
        gb = sb("gb", [P, E])
        b1T = sb("b1T", [P, PAIRS * HC * 2])
        Win = sb("Win", [P, 2 * C2 * P])
        vrow = sb("vrow", [8, C2 * P])
        vcol = sb("vcol", [P, C2, 8])
        Wx = sb("Wx", [P, C2, DTR + 2 * NS])
        diagD = sb("diagD", [P, C2, P])
        Wdt = sb("Wdt", [DTR, C2 * P])
        Wout = sb("Wout", [P, C2, D])
        An = sb("An", [P, C2, NS])
        sel = sb("sel", [P, 2 * NS, P], BF)
        stack = sb("stack", [P, T], BF)
        st = sb("st", [P, NI, 6])
        mv = sb("mv", [P, NI, 2])
        rstd = sb("rstd", [P, NI])
        rs = sb("rs", [P, 3, NI])
        nmr = sb("nmr", [P, NI])
        gate = sb("gate", [P, NI, K])
        gsum = sb("gsum", [P, NI])
        low = sb("low", [P, K, NI], BF)
        diag_p = sb("diag_p", [P, P], BF)
        diag_m = sb("diag_m", [P, P], BF)
        ixb = sb("ixb", [P, K, NI], BF)
        cf = sb("cf", [P, PAIRS])
        ci = sb("ci", [P, PAIRS], I32)
        si = sb("si", [P, PAIRS], I32)
        sf = sb("sf", [P, PAIRS])
        rf = sb("rf", [P, 3, PAIRS])
        tok_idx = sb("tok_idx", [P, PAIRS], I32)
        row_idx = sb("row_idx", [P, PAIRS], I32)

        small = stack[:, :].bitcast(FP)
        rows = small[0:E, 0:H]
        m8 = small[:, 640:896].rearrange("p (i k) -> p i k", k=8)
        ix8 = small[:, 896:1152].bitcast(U32).rearrange("p (i k) -> p i k", k=8)
        cand = small[:, 1152:1280]
        slots = small[0:E, 1280:1344]
        slots2 = small[0:E, 1344:1600].rearrange("p (a n) -> p a n", a=2)

        XN = R1[:, :].rearrange("p (i d) -> p i d", d=D)
        XT = R2[:, :]
        w1s = [BIG[:, 2048 * s:2048 * s + 1024].rearrange("p (a h) -> p a h", a=2) for s in range(RING)]
        w2s = [BIG[:, 2048 * s + 1024:2048 * s + 2048].rearrange("p (a c d) -> p a c d", a=2, c=HC)
               for s in range(RING)]
        B0 = 2048 * RING
        L = BIG[:, B0:B0 + 2048].rearrange("p (i e) -> p i e", e=E)
        V = [BIG[:, B0 + 2048 + 1024 * k:B0 + 3072 + 1024 * k].bitcast(BF)
             .rearrange("p (e i) -> p e i", i=NI) for k in range(2 * K)]
        VT = R2[:, 0:2048]
        B1 = B0 + 8192
        hs = [BIG[:, B1 + 512 * u:B1 + 512 * u + 512] for u in range(2)]
        hb = [BIG[:, B1 + 1024 + 512 * u:B1 + 1536 + 512 * u] for u in range(2)]
        hT = [BIG[:, B1 + 2048 + 512 * u:B1 + 2560 + 512 * u].rearrange("p (c n) -> p c n", c=HC)
              for u in range(2)]
        xt = [BIG[:, B1 + 3072 + 128 * u:B1 + 3200 + 128 * u] for u in range(2)]
        yo = [BIG[:, B1 + 3328 + 128 * s:B1 + 3456 + 128 * s] for s in range(RING)]
        b2s = [BIG[:, B1 + 4352 + 128 * s:B1 + 4480 + 128 * s] for s in range(RING)]
        B2 = B1 + 4352 + 128 * RING
        iotaE = BIG[:, B2:B2 + 1024].bitcast(BF).rearrange("p (e i) -> p e i", i=NI)
        assert B2 + 1024 <= 32768
        xg = [R1[:, 128 * s:128 * s + 128] for s in range(RING)]
        YK = BIG[:, 0:K * 4096].rearrange("p (k i d) -> p k i d", k=K, d=D)
        DT, DTU, HH, SG = [BIG[:, 8192 * m:8192 * m + 8192].rearrange("p (h t) -> p h t", h=C2)
                           for m in range(4)]
        pad = BIG[:, 0:2 * C2 * 2 * 259].rearrange("p (u h b t) -> p u h b t", u=2, h=C2, b=2)
        cv = BIG[:, 4200:4200 + 2 * C2 * CH].rearrange("p (u h t) -> p u h t", u=2, h=C2)
        ts = R1[0:DTR, 0:2 * CH].rearrange("p (u t) -> p u t", u=2)
        bcr = R1[32:64, 1024:2048].rearrange("p (u t) -> p u t", u=2)
        sp = R1[:, 2048:4096].rearrange("p (u h t) -> p u h t", u=2, h=C2)
        rl = R2[:, 0:2048].rearrange("p (u h t) -> p u h t", u=2, h=C2)
        dA = R1[:, 0:2048].rearrange("p (u h b t) -> p u h b t", u=2, h=C2, b=2)
        stt = R1[:, 2048:4096].rearrange("p (u h t) -> p u h t", u=2, h=C2)
        prod = R2[:, 0:2048].rearrange("p (u h t) -> p u h t", u=2, h=C2)
        Cs = R2[:, 2048:3072].rearrange("p (u t) -> p u t", u=2)
        CRED = 2
        ps = ctx.enter_context(nc.psum_tensor("ps", [P, 8, 512], FP))

        G = Sems(ctx, nc, "g")
        M = Sems(ctx, nc, "m")
        moe_sems, ln_sems = Sems(ctx, nc, "e"), Sems(ctx, nc, "l")
        F = [moe_sems.again(n, MOE_TOTALS) for n in range(2)]
        LNS = [ln_sems.again(n, LN_TOTALS) for n in range(3)]

        w1v = w1.rearrange("(a j) d h -> j d a h", a=2)
        w2v = w2.rearrange("(a j) (p c) d -> j p a (c d)", a=2, c=HC)

        def ln_vector(e, S, stats_wait=None):
            for i in range(NI):
                if stats_wait:
                    stats_wait(i)
                nc.vector.bn_stats(st[:, i, :], X[:, i, :]).then_inc(S("stats"), 1)
            for i in range(NI):
                e.wait_ge(*S.at("stats", i + 1))
                nc.vector.bn_aggr(mv[:, i, :], st[:, i, :]).then_inc(S("meanvar"), 1)
            n = 0

            def step(instruction):
                nonlocal n
                n += 1
                instruction.then_inc(S("rstd"), 1)
                e.wait_ge(*S.at("rstd", n))

            v, y, z = rs[:, 0, :], rs[:, 1, :], rs[:, 2, :]
            e.wait_ge(*S.at("meanvar", NI))
            step(nc.vector.tensor_scalar(v, mv[:, :, 1], EPS, None, ALU.add))
            step(nc.vector.tensor_single_scalar(z.bitcast(I32), v.bitcast(I32), 1, ALU.arith_shift_right))
            step(nc.vector.tensor_scalar(rstd[:, :].bitcast(I32), z.bitcast(I32), -1.0, float(0x5F3759DF),
                                         ALU.mult, ALU.add))
            for k in range(4):
                step(nc.vector.tensor_tensor(y, rstd[:, :], rstd[:, :], ALU.mult))
                step(nc.vector.scalar_tensor_tensor(out=z, in0=y, scalar=-0.5, in1=v, op0=ALU.mult, op1=ALU.mult))
                step(nc.vector.scalar_tensor_tensor(out=rstd[:, :], in0=z, scalar=1.5, in1=rstd[:, :],
                                                    op0=ALU.add, op1=ALU.mult))
            step(nc.vector.scalar_tensor_tensor(out=nmr[:, :], in0=mv[:, :, 0], scalar=-1.0, in1=rstd[:, :],
                                                op0=ALU.mult, op1=ALU.mult))
            for i in range(NI):
                if i % 4 < 3:
                    nc.vector.tensor_scalar(XN[:, i, :], X[:, i, :], mv[:, i, 0:1], rstd[:, i:i + 1],
                                            ALU.subtract, ALU.mult).then_inc(S("normed"), 1)

        def ln_scalar(e, S):
            e.wait_ge(*S.at("rstd", LN_TOTALS["rstd"]))
            for i in range(3, NI, 4):
                nc.scalar.activation(XN[:, i, :], X[:, i, :], ACT.Identity, bias=nmr[:, i:i + 1],
                                     scale=rstd[:, i:i + 1]).then_inc(S("normed_act"), 1)

        def ln_transpose(e, S, g):
            e.wait_ge(*S.at("normed", 3 * g + 3))
            e.wait_ge(*S.at("normed_act", g + 1))
            if g >= 2:
                e.wait_ge(*S.at("xT", g - 1))
            for k in range(4):
                last = nc.tensor.transpose(ps[:, g % 2, k * P:(k + 1) * P], XN[:, 4 * g + k, :], ident[:, :])
            last.then_inc(S("transposed"), 1)

        def ln_copy(e, S, g, in_time_order):
            e.wait_ge(*S.at("transposed", g + 1))
            src = ps[:, g % 2, :].rearrange("d (k p) -> d k p", k=4)
            if in_time_order:
                dst = XT.rearrange("d (p i) -> d i p", i=NI)[:, 4 * g:4 * g + 4, :]
            else:
                dst = XT.rearrange("d (i p) -> d i p", i=NI)[:, 4 * g:4 * g + 4, :]
            nc.scalar.activation(dst, src, ACT.Copy).then_inc(S("xT"), 1)

        def moe_sync(e, S, f):
            def load_w1(r, s):
                j = RING * r + s
                e.dma_start(w1s[s], w1v[bass.ds(j, 1)].rearrange("o d a h -> (o d) a h")).then_inc(G(f"w1_{s}"), 16)

            def load_w2(r, s):
                j = RING * r + s
                e.dma_start(BIG[:, 2048 * s + 1024:2048 * s + 2048].rearrange("p (a h) -> p a h", a=2),
                            w2v[bass.ds(j, 1)].rearrange("o p a h -> (o p) a h")).then_inc(G(f"w2_{s}"), 16)
                for a in range(2):
                    e.dma_start(b2s[s][a * CAP:(a + 1) * CAP, :],
                                b2[bass.ds(j + PAIRS * a, 1), :].broadcast_to([CAP, D])).then_inc(G(f"b2_{s}"), 16)

            for s in range(RING):
                load_w1(0, s)
                load_w2(0, s)
            if f == 0:
                for k in range(K):
                    e.dma_start(y_dram[0][k * T:(k + 1) * T, :].rearrange("(p a i) d -> p a (i d)", p=P, a=8),
                                zeros[:, :].unsqueeze(1).broadcast_to([P, 8, 512])).then_inc(S("zeroed"), 16)
            with e.Fori(1, ROUNDS) as r:
                for s in range(RING):
                    e.wait_ge(*S.at("h_psum", RING * r + s - RING + 1))
                    load_w1(r, s)
                    e.wait_ge(*S.at("y_psum", RING * r + s - RING + 1))
                    e.wait_ge(*S.at("yo", RING * r + s - RING + 1))
                    load_w2(r, s)
            e.wait_ge(*S.at("y_psum", PAIRS))
            for s in range(RING):
                e.wait_ge(G(f"scattered{s}"), 16 * ROUNDS * (f + 1))
            yv = y_dram[f].rearrange("(k p i) d -> k p i d", k=K, p=P)
            for q in range(4):
                for k in range(K):
                    e.dma_start(YK[:, k, 8 * q:8 * q + 8, :], yv[k, :, 8 * q:8 * q + 8, :])\
                        .then_inc(G(f"yk{q}"), 16)

        def moe_scalar(e, S, LS, f):
            ln_scalar(e, LS)
            for g in range(8):
                ln_copy(e, LS, g, False)
            for b in range(4):
                e.wait_ge(*S.at("codesT", b + 1))
                nc.scalar.activation(VT[:, 512 * b:512 * b + 512], ps[:, 4 + b, :], ACT.Copy).then_inc(S("VT"), 1)
            e.wait_ge(*S.at("mdiff", 1))
            nc.scalar.activation(gate[:, :, :], gate[:, :, :], ACT.Exp).then_inc(S("gexp"), 1)

            def xt_copy(j, s, r):
                e.wait_ge(*S.at("x_psum", j + 1))
                if not (type(j) is int and j < 2):
                    e.wait_ge(*S.at("h_psum", j - 1))
                nc.scalar.activation(xt[s % 2], ps[:, 7 * (s % 2), 0:P], ACT.Copy).then_inc(S("xt"), 1)

            def gelu(j, s, r):
                e.wait_ge(*S.at("hb", j + 1))
                if not (type(j) is int and j < 2):
                    e.wait_ge(*S.at("y_psum", j - 1))
                nc.scalar.activation(hT[s % 2].rearrange("p c n -> p (c n)"), hb[s % 2], ACT.Gelu)\
                    .then_inc(S("hT"), 1)

            for j in range(3):
                xt_copy(j, j, 0)
            gelu(0, 0, 0)
            pipeline(e, RING, ROUNDS, [(3, xt_copy), (1, gelu)])

        def pipeline(e, ring, rounds, stages):
            def one(r):
                for s in range(ring):
                    for lead, do in stages:
                        j, slot, rr = ring * r + s + lead, (s + lead) % ring, r
                        if s + lead < 0:
                            rr = r - 1
                        elif s + lead >= ring:
                            rr = r + 1
                        if type(r) is int and not 0 <= j < ring * rounds:
                            continue
                        do(j, slot, rr)
            one(0)
            with e.Fori(1, rounds - 1) as r:
                one(r)
            one(rounds - 1)

        def moe_tensor(e, S, LS, f):
            def logits(g):
                e.wait_ge(*LS.at("xT", 2 * g + 2))
                if g >= 2:
                    e.wait_ge(*S.at("L", g - 1))
                for k in range(8):
                    i = 8 * g + k
                    last = nc.tensor.matmul(ps[:, 2 + g % 2, E * k:E * k + E], XT[:, i * P:i * P + P], gw[:, :],
                                            start=True, stop=True)
                last.then_inc(S("logits"), 1)

            for g in range(8):
                ln_transpose(e, LS, g)
                if g >= 3 and g % 2 == 1:
                    logits((g - 3) // 2)
            logits(3)
            for k in range(2 * K):
                e.wait_ge(*S.at("V", k + 1))
            for g in range(16):
                for k in range(2 * K):
                    last = nc.tensor.matmul(ps[:, 4 + g // 4, (g % 4) * P:(g % 4 + 1) * P],
                                            V[k].rearrange("p e (f g) -> p g (e f)", f=2)[:, g, :],
                                            (diag_p if k < K else diag_m)[:, :],
                                            start=(k == 0), stop=(k == 2 * K - 1))
                if g % 4 == 3:
                    last.then_inc(S("codesT"), 1)
            e.wait_ge(*S.at("cand", 16))
            for a in range(2):
                last = nc.tensor.matmul(ps[0:E, 2, a * CAP:(a + 1) * CAP],
                                        ident[:, :].rearrange("p (e a) -> p a e", a=2)[:, a, :], cand[:, 0:CAP],
                                        start=True, stop=True)
            last.then_inc(S("moved"), 1)
            e.wait_ge(*S.at("slots2", 2))
            nc.tensor.matmul(ps[:, 3, 0:PAIRS], slots2[:, 0, :], ident[0:E, 0:PAIRS], start=True, stop=False)
            nc.tensor.matmul(ps[:, 3, 0:PAIRS], slots2[:, 1, :], ident[0:E, PAIRS:E], start=False, stop=True)\
                .then_inc(S("slotcode"), 1)

            def later(j):
                return not (type(j) is int and j < 2)

            def t_in(j, s, r):
                e.wait_ge(G(f"gathered{s}"), 16 * (ROUNDS * f + r + 1))
                if later(j):
                    e.wait_ge(*S.at("xt", j - 1))
                nc.tensor.transpose(ps[:, 7 * (s % 2), 0:P], xg[s], ident[:, :]).then_inc(S("x_psum"), 1)

            def mm1(j, s, r):
                e.wait_ge(*S.at("xt", j + 1))
                e.wait_ge(G(f"w1_{s}"), 16 * (ROUNDS * f + r + 1))
                if later(j):
                    e.wait_ge(*S.at("hs", j - 1))
                for a in range(2):
                    last = nc.tensor.matmul(ps[a * CAP:(a + 1) * CAP, 1 + s % 2, :], xt[s % 2][:, a * CAP:(a + 1) * CAP],
                                            w1s[s][:, a, :], start=True, stop=True)
                last.then_inc(S("h_psum"), 1)

            def ht(j, s, r):
                e.wait_ge(*S.at("hs", j + 1))
                if later(j):
                    e.wait_ge(*S.at("hb", j - 1))
                for c in range(HC):
                    last = nc.tensor.transpose(ps[:, 3 + s % 2, c * P:(c + 1) * P],
                                               hs[s % 2].rearrange("n (p c) -> n c p", c=HC)[:, c, :], ident[:, :])
                last.then_inc(S("ht_psum"), 1)

            def mm2(j, s, r):
                e.wait_ge(*S.at("hT", j + 1))
                e.wait_ge(G(f"w2_{s}"), 16 * (ROUNDS * f + r + 1))
                if later(j):
                    e.wait_ge(*S.at("yo", j - 1))
                for c in range(HC):
                    for a in range(2):
                        last = nc.tensor.matmul(ps[a * CAP:(a + 1) * CAP, 5 + s % 2, 0:D],
                                                hT[s % 2][:, c, a * CAP:(a + 1) * CAP], w2s[s][:, a, c, :],
                                                start=(c == 0), stop=(c == HC - 1))
                last.then_inc(S("y_psum"), 1)

            t_in(0, 0, 0)
            t_in(1, 1, 0)
            mm1(0, 0, 0)
            t_in(2, 2, 0)
            mm1(1, 1, 0)
            ht(0, 0, 0)
            pipeline(e, RING, ROUNDS, [(3, t_in), (2, mm1), (1, ht), (0, mm2)])

        def moe_vector(e, S, LS, f, stats_wait=None):
            ln_vector(e, LS, stats_wait)
            for g in range(4):
                e.wait_ge(*S.at("logits", g + 1))
                nc.vector.tensor_tensor(L[:, 8 * g:8 * g + 8, :],
                                        ps[:, 2 + g % 2, :].rearrange("p (i e) -> p i e", e=E),
                                        gb[:, :].unsqueeze(1).broadcast_to([P, 8, E]), ALU.add).then_inc(S("L"), 1)
            for g in range(4):
                e.wait_ge(*S.at("L", g + 1))
                for i in range(8 * g, 8 * g + 8):
                    nc.vector.max(m8[:, i, :], L[:, i, :]).then_inc(S("m8"), 1)
            for i in range(NI):
                e.wait_ge(*S.at("m8", i + 1))
                nc.vector.max_index(ix8[:, i, :], m8[:, i, :], L[:, i, :]).then_inc(S("ix8"), 1)
            e.wait_ge(*S.at("ix8", NI))
            nc.vector.tensor_copy(ixb[:, :, :].rearrange("p k i -> p i k"), ix8[:, :, 0:K]).then_inc(S("ixf"), 1)
            nc.vector.tensor_tensor(gate[:, :, :], m8[:, :, 0:K], m8[:, :, 0:1].broadcast_to([P, NI, K]),
                                    ALU.subtract).then_inc(S("mdiff"), 1)
            e.wait_ge(*S.at("ixf", 1))
            e.wait_ge(G("code"), 4 + f)
            for k in range(K):
                nc.vector.tensor_tensor(V[k], iotaE, ixb[:, k, :].unsqueeze(1).broadcast_to([P, E, NI]),
                                        ALU.is_equal).then_inc(S("V"), 1)
            for k in range(K):
                e.wait_ge(*S.at("V", k + 1))
                nc.vector.tensor_tensor(V[K + k], V[k], low[:, k, :].unsqueeze(1).broadcast_to([P, E, NI]),
                                        ALU.mult).then_inc(S("V"), 1)
            e.wait_ge(*S.at("gexp", 1))
            nc.vector.reduce_sum(gsum[:, :], gate[:, :, :], axis=mybir.AxisListType.X).then_inc(S("gs"), 1)
            e.wait_ge(*S.at("gs", 1))
            nc.vector.reciprocal(gsum[:, :], gsum[:, :]).then_inc(S("gs"), 1)
            e.wait_ge(*S.at("gs", 2))
            nc.vector.scalar_tensor_tensor(out=gate[:, :, :], in0=gate[:, :, :], scalar=0.5,
                                           in1=gsum[:, :].unsqueeze(2).broadcast_to([P, NI, K]),
                                           op0=ALU.mult, op1=ALU.mult).then_inc(S("gs"), 1)
            e.wait_ge(*S.at("VT", 4))
            for r in range(CAP // 8):
                if r:
                    e.wait_ge(*S.at("cand", 2 * r))
                c8 = cand[:, 8 * r:8 * r + 8]
                nc.vector.max(c8, VT).then_inc(S("cand"), 1)
                e.wait_ge(*S.at("cand", 2 * r + 1))
                nc.vector.match_replace(VT, c8, VT, 0.0).then_inc(S("cand"), 1)
            e.wait_ge(*S.at("moved", 1))
            nc.vector.tensor_copy(cand[0:E, :], ps[0:E, 2, 0:2 * CAP]).then_inc(S("merged"), 1)
            for r in range(CAP // 8):
                e.wait_ge(*S.at("merged", 2 * r + 1))
                c8 = slots[:, 8 * r:8 * r + 8]
                nc.vector.max(c8, cand[0:E, :]).then_inc(S("merged"), 1)
                e.wait_ge(*S.at("merged", 2 * r + 2))
                nc.vector.match_replace(cand[0:E, :], c8, cand[0:E, :], 0.0).then_inc(S("merged"), 1)
            nc.vector.memset(slots2[:, :, :], 0.0).then_inc(S("slots2_zero"), 1)
            e.wait_ge(*S.at("slots2_zero", 1))
            e.wait_ge(*S.at("merged", 2 * (CAP // 8) + 1))
            for a in range(2):
                nc.vector.tensor_copy(slots2[:, a, a * CAP:(a + 1) * CAP], slots[:, :]).then_inc(S("slots2"), 1)
            n = 0

            def dec(instruction):
                nonlocal n
                n += 1
                instruction.then_inc(S("decode"), 1)
                e.wait_ge(*S.at("decode", n))

            e.wait_ge(*S.at("slotcode", 1))
            dec(nc.vector.tensor_copy(cf[:, :], ps[:, 3, 0:PAIRS]))
            dec(nc.vector.tensor_scalar(ci[:, :], cf[:, :], 3.0, None, ALU.add))
            dec(nc.vector.tensor_single_scalar(si[:, :], ci[:, :], 2, ALU.arith_shift_right))
            dec(nc.vector.tensor_copy(sf[:, :], si[:, :]))
            dec(nc.vector.tensor_scalar(rf[:, 0, :], sf[:, :], -1.0, float(T), ALU.mult, ALU.add))
            dec(nc.vector.tensor_scalar(tok_idx[:, :], rf[:, 0, :], float(T - 1), None, ALU.min))
            dec(nc.vector.scalar_tensor_tensor(out=rf[:, 1, :], in0=sf[:, :], scalar=4.0, in1=cf[:, :],
                                               op0=ALU.mult, op1=ALU.subtract))
            dec(nc.vector.scalar_tensor_tensor(out=rf[:, 2, :], in0=rf[:, 1, :], scalar=float(T), in1=rf[:, 0, :],
                                               op0=ALU.mult, op1=ALU.add))
            dec(nc.vector.tensor_scalar(rf[:, 1, :], cf[:, :], 0.0, float(2 * K * T), ALU.is_equal, ALU.mult))
            dec(nc.vector.tensor_tensor(row_idx[:, :], rf[:, 2, :], rf[:, 1, :], ALU.add))

            def later(j):
                return not (type(j) is int and j < 2)

            def h_copy(j, s, r):
                e.wait_ge(*S.at("h_psum", j + 1))
                if later(j):
                    e.wait_ge(*S.at("ht_psum", j - 1))
                nc.vector.tensor_copy(hs[s % 2], ps[:, 1 + s % 2, :]).then_inc(S("hs"), 1)

            def bias1(j, s, r):
                e.wait_ge(*S.at("ht_psum", j + 1))
                if later(j):
                    e.wait_ge(*S.at("hT", j - 1))
                bias = b1T[:, bass.ds(2 * HC * j, 2 * HC)].unsqueeze(2).broadcast_to([P, 2 * HC, CAP])
                nc.vector.tensor_tensor(hb[s % 2].rearrange("p (c n) -> p c n", n=CAP),
                                        ps[:, 3 + s % 2, :].rearrange("p (c n) -> p c n", n=CAP), bias,
                                        ALU.add).then_inc(S("hb"), 1)

            def y_bias(j, s, r):
                e.wait_ge(*S.at("y_psum", j + 1))
                e.wait_ge(G(f"b2_{s}"), 32 * (ROUNDS * f + r + 1))
                if f or not (type(r) is int and r == 0):
                    e.wait_ge(G(f"scattered{s}"), 16 * (ROUNDS * f + r))
                nc.vector.tensor_tensor(yo[s], ps[:, 5 + s % 2, 0:D], b2s[s], ALU.add).then_inc(S("yo"), 1)

            h_copy(0, 0, 0)
            h_copy(1, 1, 0)
            bias1(0, 0, 0)
            pipeline(e, RING, ROUNDS, [(2, h_copy), (1, bias1), (0, y_bias)])
            for q in range(4):
                e.wait_ge(G(f"yk{q}"), 16 * K * (f + 1))
                for k in range(K):
                    for i in range(8 * q, 8 * q + 8):
                        if k:
                            e.wait_ge(*S.at("x", 24 * q + 8 * (k - 1) + i - 8 * q + 1))
                        nc.vector.scalar_tensor_tensor(out=X[:, i, :], in0=YK[:, k, i, :],
                                                       scalar=gate[:, i, k:k + 1], in1=X[:, i, :],
                                                       op0=ALU.mult, op1=ALU.add).then_inc(S("x"), 1)
            e.wait_ge(*S.at("x", NI * K))

        def moe_pool(e, S, LS, f):
            e.wait_ge(*LS.at("normed", 24))
            e.wait_ge(*LS.at("normed_act", 8))
            e.dma_start(xn_dram[f].rearrange("(p i) d -> p (i d)", p=P), R1[:, :]).then_inc(S("xn_stored"), 16)
            e.wait_ge(*S.at("xn_stored", 16))
            e.wait_ge(*S.at("decode", 10))

            def gather(j):
                s = j % RING
                if j >= RING:
                    e.wait_ge(*S.at("x_psum", j - RING + 1))
                nc.gpsimd.indirect_dma_start(
                    xg[s], None, xn_dram[f], bass.IndirectOffsetOnAxis(tok_idx[:, j:j + 1].bitcast(U32), 0),
                    bounds_check=T - 1, oob_is_err=False).then_inc(G(f"gathered{s}"), 16)

            for j in range(RING):
                gather(j)
            if f == 0:
                e.wait_ge(*S.at("zeroed", 16 * K))
            else:
                e.wait_ge(M("zeroed"), 16 * K)
            for j in range(PAIRS):
                s = j % RING
                e.wait_ge(*S.at("yo", j + 1))
                nc.gpsimd.indirect_dma_start(
                    y_dram[f], bass.IndirectOffsetOnAxis(row_idx[:, j:j + 1].bitcast(U32), 0), yo[s], None,
                    bounds_check=K * T - 1, oob_is_err=False).then_inc(G(f"scattered{s}"), 16)
                if j + RING < PAIRS:
                    gather(j + RING)

        def mamba_tensor(e):
            LS = LNS[1]
            for g in range(8):
                ln_transpose(e, LS, g)
            e.wait_ge(*LS.at("xT", 8))

            def raw(q, u, r):
                e.wait_ge(M("raw"), q - 2 + CRED + 1)
                for m in range(2):
                    last = nc.tensor.matmul(ps[:, 2 * u + m, :], Win[:, m * P:(m + 1) * P],
                                            XT[:, bass.ds(CH * q, CH)], start=True, stop=True)
                last.then_inc(M("raw_psum"), 1)

            def gates(q, u, r):
                e.wait_ge(M("sg"), q - 2 + CRED + 1)
                for m in range(2):
                    last = nc.tensor.matmul(ps[:, 4 + 2 * u + m, :], Win[:, (2 + m) * P:(3 + m) * P],
                                            XT[:, bass.ds(CH * q, CH)], start=True, stop=True)
                last.then_inc(M("gate_psum"), 1)

            pipeline(e, 2, NQ // 2, [(0, raw), (0, gates)])

            e.wait_ge(M("h"), NQ + CRED)
            e.wait_ge(M("sg"), NQ + CRED)

            def x_proj(q, u, r):
                e.wait_ge(M("ts"), q - 2 + CRED + 1)
                e.wait_ge(M("rest"), q - 2 + CRED + 1)
                for h in range(C2):
                    last = nc.tensor.matmul(ps[0:DTR + 2 * NS, u, :], Wx[:, h, :], HH[:, h, bass.ds(CH * q, CH)],
                                            start=(h == 0), stop=(h == C2 - 1))
                last.then_inc(M("x_psum"), 1)

            def dt_proj(q, u, r):
                e.wait_ge(M("ts"), q + 1 + CRED)
                e.wait_ge(M("z"), q - 2 + CRED + 1)
                for h in range(C2):
                    last = nc.tensor.matmul(ps[:, 2 + 2 * u + h, :], Wdt[:, h * P:(h + 1) * P], ts[:, u, :],
                                            start=True, stop=True)
                last.then_inc(M("dt_psum"), 1)

            x_proj(0, 0, 0)
            pipeline(e, 2, NQ // 2, [(1, x_proj), (0, dt_proj)])

            e.wait_ge(M("z"), NQ + CRED)
            e.wait_ge(M("stack"), NQ + CRED)
            e.wait_ge(M("diagD"), C2)

            def b_and_c(q, n):
                step = NS * q + n
                e.wait_ge(M("dbu"), 2 * (step + CRED))
                nc.tensor.matmul(ps[:, 2, :], sel[0:96, n, :], stack[0:96, bass.ds(CH * q, CH)],
                                 start=True, stop=True).then_inc(M("b_psum"), 1)
                e.wait_ge(M("cs"), step + CRED)
                nc.tensor.matmul(ps[:, 3, :], sel[0:96, NS + n, :], stack[0:96, bass.ds(CH * q, CH)],
                                 start=True, stop=True).then_inc(M("c_psum"), 1)

            def chunk(q, u, last_chunk):
                e.wait_ge(M("y"), 2 * (q - 2 + CRED) + 2)
                for h in range(C2):
                    nc.tensor.matmul(ps[:, 4 + 2 * u + h, :], diagD[:, h, :], HH[:, h, bass.ds(CH * q, CH)],
                                     start=True, stop=False)
                for n in range(NS):
                    if n < NS - 2:
                        b_and_c(q, n + 2)
                    elif not last_chunk:
                        b_and_c(q + 1, n + 2 - NS)
                    e.wait_ge(M("prod"), NS * q + n + 1 + CRED)
                    for h in range(C2):
                        last = nc.tensor.matmul(ps[:, 4 + 2 * u + h, :], ident[:, :], prod[:, n % 2, h, :],
                                                start=False, stop=(n == NS - 1))
                    last.then_inc(M("summed"), 1)

            b_and_c(0, 0)
            b_and_c(0, 1)
            with e.Fori(0, NQ // 2 - 1) as r:
                for u in range(2):
                    chunk(2 * r + u, u, False)
            for u in range(2):
                chunk(NQ - 2 + u, u, u == 1)

            e.wait_ge(M("y"), 2 * (NQ + CRED))
            for g in range(8):
                if g >= 2:
                    e.wait_ge(M("x"), g - 1)
                for k in range(4):
                    for h in range(C2):
                        lhsT = SG[:, h, :].rearrange("p (q i) -> p i q", i=NI)[:, 4 * g + k, :]
                        last = nc.tensor.matmul(ps[:, g % 2, k * P:(k + 1) * P], lhsT, Wout[:, h, :],
                                                start=(h == 0), stop=(h == C2 - 1))
                last.then_inc(M("o_psum"), 1)

        def mamba_scalar(e):
            LS = LNS[1]

            def own_wait():
                e.sem_inc(M("held"), 1)

            ln_scalar(e, LS)
            for g in range(8):
                ln_copy(e, LS, g, True)

            def raw_copy(q, u, r):
                e.wait_ge(M("raw_psum"), q + 1)
                e.wait_ge(M("conv"), q - 2 + CRED + 1)
                nc.scalar.activation(pad[:, u, :, :, 3:3 + SEQ],
                                     ps[:, 2 * u:2 * u + 2, :].rearrange("p h (b t) -> p h b t", b=2), ACT.Copy)
                e.wait_ge(M("h"), q - 2 + CRED + 1)
                for h in range(C2):
                    last = nc.scalar.activation(cv[:, u, h, :], ps[:, 2 * u + h, :], ACT.Identity,
                                                bias=vcol[:, h, 4:5], scale=vcol[:, h, 3:4])
                last.then_inc(M("raw"), 1)

            def gate_silu(q, u, r):
                e.wait_ge(M("gate_psum"), q + 1)
                own_wait()
                nc.scalar.activation(SG[:, :, bass.ds(CH * q, CH)], ps[:, 4 + 2 * u:6 + 2 * u, :], ACT.Silu)\
                    .then_inc(M("sg"), 1)

            def h_silu(q, u, r):
                e.wait_ge(M("conv"), q + 1 + CRED)
                own_wait()
                nc.scalar.activation(HH[:, :, bass.ds(CH * q, CH)], cv[:, u, :, :], ACT.Silu).then_inc(M("h"), 1)

            raw_copy(0, 0, 0)
            pipeline(e, 2, NQ // 2, [(-1, h_silu), (1, raw_copy), (0, gate_silu)])
            h_silu(NQ - 1, 1, NQ // 2 - 1)

            def x_parts(q, u, r):
                e.wait_ge(M("x_psum"), q + 1)
                e.wait_ge(M("dt_psum"), q - 2 + CRED + 1)
                nc.scalar.activation(ts[:, u, :], ps[0:DTR, u, :], ACT.Copy).then_inc(M("ts"), 1)
                nc.scalar.activation(stack[0:32, bass.ds(CH * q, CH)], ps[DTR:DTR + 2 * NS, u, :], ACT.Copy)\
                    .then_inc(M("hi"), 1)

            def mid(q, u, r):
                e.wait_ge(M("rest"), q + 1 + CRED)
                own_wait()
                nc.scalar.activation(stack[32:64, bass.ds(CH * q, CH)], bcr[:, u, :], ACT.Copy).then_inc(M("mid"), 1)

            def softplus(q, u, r):
                e.wait_ge(M("z"), q + 1 + CRED)
                e.wait_ge(M("dt"), q - 2 + CRED + 1)
                nc.scalar.activation(sp[:, u], rl[:, u], ACT.Abs).then_inc(M("abs"), 1)
                e.wait_ge(M("abs"), q + 1)
                nc.scalar.activation(sp[:, u], sp[:, u], ACT.Exp, scale=-1.0).then_inc(M("exp"), 1)
                e.wait_ge(M("exp"), q + 1)
                nc.scalar.activation(sp[:, u], sp[:, u], ACT.Ln, bias=1.0).then_inc(M("ln"), 1)

            x_parts(0, 0, 0)
            mid(0, 0, 0)
            pipeline(e, 2, NQ // 2, [(1, x_parts), (0, softplus), (1, mid)])

            e.wait_ge(M("dt"), NQ + CRED)
            e.wait_ge(M("stack"), NQ + CRED)
            e.wait_ge(M("dA_zero"), 1)
            with e.Fori(0, NQ) as q:
                for n in range(NS):
                    step = NS * q + n
                    e.wait_ge(M("scanned"), 2 * (step - 2 + CRED) + 2)
                    own_wait()
                    for h in range(C2):
                        nc.scalar.activation(
                            dA[:, n % 2, h, :, 1:SEQ],
                            DT[:, h, bass.ds(CH * q, CH)].rearrange("p (b t) -> p b t", b=2)[:, :, 1:SEQ],
                            ACT.Exp, scale=An[:, h, n:n + 1]).then_inc(M("dA"), 1)
                    e.wait_ge(M("c_psum"), step + 1)
                    e.wait_ge(M("prod"), step - 2 + CRED + 1)
                    nc.scalar.activation(Cs[:, n % 2, :], ps[:, 3, :], ACT.Copy).then_inc(M("cs"), 1)

        def mamba_vector(e):
            ln_vector(e, LNS[1])

            def conv(q, u, r):
                e.wait_ge(M("raw"), q + 1 + CRED)
                for k in range(KC - 1):
                    for h in range(C2):
                        o = cv[:, u, h, :].rearrange("p (b t) -> p b t", b=2)
                        if k:
                            e.wait_ge(M("tap"), (KC - 1) * C2 * q + C2 * (k - 1) + h + 1)
                        last = nc.vector.scalar_tensor_tensor(out=o, in0=pad[:, u, h, :, k:k + SEQ],
                                                              scalar=vcol[:, h, k:k + 1], in1=o,
                                                              op0=ALU.mult, op1=ALU.add)
                        last.then_inc(M("tap"), 1)
                e.wait_ge(M("tap"), (KC - 1) * C2 * (q + 1))
                e.sem_inc(M("conv"), 1)

            pipeline(e, 2, NQ // 2, [(0, conv)])

            def rest(q, u, r):
                e.wait_ge(M("hi"), q + 1)
                e.wait_ge(M("stack"), q - 2 + CRED + 1)
                nc.vector.tensor_tensor(bcr[:, u, :], ps[DTR:DTR + 2 * NS, u, :], stack[0:32, bass.ds(CH * q, CH)],
                                        ALU.subtract).then_inc(M("rest"), 1)

            def z(q, u, r):
                e.wait_ge(M("dt_psum"), q + 1 + CRED)
                e.wait_ge(M("dt"), q - 2 + CRED + 1)
                for h in range(C2):
                    last = nc.vector.tensor_scalar(rl[:, u, h, :], ps[:, 2 + 2 * u + h, :], vcol[:, h, 5:6], None,
                                                   ALU.add)
                last.then_inc(M("z"), 1)

            def dt(q, u, r):
                e.wait_ge(M("ln"), q + 1)
                nc.vector.scalar_tensor_tensor(out=DT[:, :, bass.ds(CH * q, CH)], in0=rl[:, u], scalar=0.0,
                                               in1=sp[:, u], op0=ALU.max, op1=ALU.add).then_inc(M("dt"), 1)

            rest(0, 0, 0)
            z(0, 0, 0)
            pipeline(e, 2, NQ // 2, [(1, rest), (1, z), (0, dt)])

            e.wait_ge(M("dtu"), NQ + CRED)

            def y_out(q, u):
                e.wait_ge(M("summed"), NS * q + NS + CRED)
                for h in range(C2):
                    nc.vector.tensor_tensor(SG[:, h, bass.ds(CH * q, CH)], ps[:, 4 + 2 * u + h, :],
                                            SG[:, h, bass.ds(CH * q, CH)], ALU.mult).then_inc(M("y"), 1)

            def chunk(q, u, first):
                for n in range(NS):
                    step = NS * q + n
                    e.wait_ge(M("b_psum"), step + 1)
                    for h in range(C2):
                        e.wait_ge(M("scanned"), 2 * (step - 1 + CRED) + h + 1)
                        nc.vector.tensor_tensor(ps[:, h, :], DTU[:, h, bass.ds(CH * q, CH)], ps[:, 2, :],
                                                ALU.mult).then_inc(M("dbu"), 1)
                    e.wait_ge(M("prod"), step - 2 + CRED + 1)
                    for h in range(C2):
                        e.wait_ge(M("dbu"), 2 * (step + CRED) + h + 1)
                        e.wait_ge(M("dA"), 2 * step + h + 1)
                        nc.vector.tensor_tensor_scan(stt[:, n % 2, h, :],
                                                     dA[:, n % 2, h, :, :].rearrange("p b t -> p (b t)"),
                                                     ps[:, h, :], 0.0, ALU.mult, ALU.add)\
                            .then_inc(M("scanned"), 1)
                    if n == 3 and not first:
                        y_out(q - 1, 1 - u)

            for u in range(2):
                chunk(u, u, u == 0)
            with e.Fori(1, NQ // 2) as r:
                for u in range(2):
                    chunk(2 * r + u, u, False)
            y_out(NQ - 1, 1)
            for g in range(8):
                e.wait_ge(M("o_psum"), g + 1)
                nc.vector.tensor_tensor(X[:, 4 * g:4 * g + 4, :].rearrange("p i d -> p (i d)"),
                                        X[:, 4 * g:4 * g + 4, :].rearrange("p i d -> p (i d)"), ps[:, g % 2, :],
                                        ALU.add).then_inc(M("x"), 1)
            e.wait_ge(M("x"), 8)

        def mamba_pool(e):
            def lo(q, u, r):
                e.wait_ge(M("mid"), q + 1)
                e.wait_ge(M("dtu"), q + CRED)
                nc.gpsimd.tensor_tensor(stack[64:96, bass.ds(CH * q, CH)], bcr[:, u, :],
                                        stack[32:64, bass.ds(CH * q, CH)], ALU.subtract).then_inc(M("stack"), 1)

            def dtu(q, u, r):
                e.wait_ge(M("stack"), q + 1 + CRED)
                e.wait_ge(M("dt"), q + 1 + CRED)
                nc.gpsimd.tensor_tensor(DTU[:, :, bass.ds(CH * q, CH)], DT[:, :, bass.ds(CH * q, CH)],
                                        HH[:, :, bass.ds(CH * q, CH)], ALU.mult).then_inc(M("dtu"), 1)

            lo(0, 0, 0)
            pipeline(e, 2, NQ // 2, [(0, dtu), (1, lo)])
            e.wait_ge(M("dtu"), NQ + CRED)
            nc.gpsimd.memset(dA[:, :, :, :, 0:1], 0.0).then_inc(M("dA_zero"), 1)
            e.wait_ge(M("dA_zero"), 1)
            with e.Fori(0, NQ) as q:
                for n in range(NS):
                    step = NS * q + n
                    e.wait_ge(M("scanned"), 2 * (step + CRED) + 2)
                    e.wait_ge(M("cs"), step + CRED + 1)
                    e.wait_ge(M("summed"), step - 2 + CRED + 1)
                    nc.gpsimd.tensor_tensor(prod[:, n % 2], stt[:, n % 2],
                                            Cs[:, n % 2, :].unsqueeze(1).broadcast_to([P, C2, CH]),
                                            ALU.mult).then_inc(M("prod"), 1)

        block = ctx.enter_context(nc.Block())

        @block.sync
        def _(e):
            xv = x_in.rearrange("b (c i) d -> (b c) i d", i=NI)
            for q in range(4):
                e.dma_start(X[:, 8 * q:8 * q + 8, :], xv[:, 8 * q:8 * q + 8, :]).then_inc(G(f"x{q}"), 16)
            e.dma_start(gw[:, :], gate_w).then_inc(G("gw"), 16)
            e.dma_start(gb[:, :], gate_b.rearrange("(a n) -> a n", a=1).broadcast_to([P, E])).then_inc(G("gb"), 16)
            e.dma_start(rows, b1).then_inc(G("rows"), 16)
            e.wait_ge(G("zeros"), 1)
            moe_sync(e, F[0], 0)
            e.dma_start(Win[:, :], W_in).then_inc(G("mw"), 16)
            e.dma_start(Wx[:, :, :], W_x.rearrange("(h p) n -> p h n", p=P)).then_inc(G("mw"), 16)
            e.dma_start(Wdt[:, :], W_dt).then_inc(G("mw"), 16)
            e.dma_start(Wout[:, :, :], W_out.rearrange("(h p) n -> p h n", p=P)).then_inc(G("mw"), 16)
            e.dma_start(An[:, :, :], A_log.rearrange("(h p) n -> p h n", p=P)).then_inc(G("mw"), 16)
            e.dma_start(vrow[0:KC, :], conv_w.rearrange("k o c -> k (o c)")).then_inc(G("mw"), 16)
            for k, v in enumerate((conv_b, b_dt, D_w)):
                e.dma_start(vrow[KC + k:KC + k + 1, :], v.rearrange("(a c) -> a c", a=1)).then_inc(G("mw"), 16)
            for k in range(K):
                e.dma_start(y_dram[1][k * T:(k + 1) * T, :].rearrange("(p a i) d -> p a (i d)", p=P, a=8),
                            zeros[:, :].unsqueeze(1).broadcast_to([P, 8, 512])).then_inc(M("zeroed"), 16)
            e.wait_ge(M("o_psum"), 8)
            moe_sync(e, F[1], 1)
            for q in range(4):
                e.wait_ge(*F[1].at("x", 24 * q + 24))
                e.dma_start(out.rearrange("b (c i) d -> (b c) i d", i=NI)[:, 8 * q:8 * q + 8, :],
                            X[:, 8 * q:8 * q + 8, :]).then_inc(G("out"), 16)
            e.wait_ge(G("out"), 64)

        @block.gpsimd
        def _(e):
            def expert_numbers():
                nc.gpsimd.iota(iotaE, pattern=[[1, E], [0, NI]], base=0, channel_multiplier=0,
                               allow_small_or_imprecise_dtypes=True).then_inc(G("code"), 1)

            nc.gpsimd.memset(ident[:, :], 0.0).then_inc(G("id0"), 1)
            nc.gpsimd.memset(zeros[:, :], 0.0).then_inc(G("zeros"), 1)
            e.wait_ge(G("id0"), 1)
            nc.gpsimd.affine_select(out=ident[:, :], in_=ident[:, :], compare_op=ALU.not_equal, fill=1.0, base=0,
                                    pattern=[[-1, P]], channel_multiplier=1).then_inc(G("ident"), 1)
            expert_numbers()
            nc.gpsimd.iota(low[:, :, :], pattern=[[1, K], [4, NI]], base=0, channel_multiplier=0,
                           allow_small_or_imprecise_dtypes=True).then_inc(G("code"), 1)
            nc.gpsimd.iota(diag_p[:, :], pattern=[[0, P]], base=4 * T, channel_multiplier=-4 * NI,
                           allow_small_or_imprecise_dtypes=True).then_inc(G("diag"), 1)
            nc.gpsimd.memset(diag_m[:, :], -1.0).then_inc(G("diag"), 1)
            for k, m in enumerate((diag_p, diag_m)):
                e.wait_ge(G("diag"), 2)
                nc.gpsimd.affine_select(out=m[:, :], in_=m[:, :], compare_op=ALU.is_equal, fill=0.0, base=0,
                                        pattern=[[-1, P]], channel_multiplier=1).then_inc(G("code"), 1)
            nc.gpsimd.memset(sel[:, :, :], 0.0).then_inc(G("sel0"), 1)
            nc.gpsimd.memset(vrow[:, :], 0.0).then_inc(G("vrow0"), 1)
            for name, c in (("raw", CRED), ("sg", CRED), ("conv", CRED), ("h", CRED), ("ts", CRED), ("rest", CRED),
                            ("z", CRED), ("dt_psum", CRED), ("stack", CRED), ("dt", CRED), ("dtu", CRED),
                            ("prod", CRED), ("scanned", 2 * CRED), ("summed", CRED), ("dbu", 2 * CRED),
                            ("cs", CRED), ("y", 2 * CRED)):
                e.sem_inc(M(name), c)
            e.wait_ge(G("sel0"), 1)
            for g in range(3):
                e.wait_ge(G("sel"), g)
                part = sel[32 * g:32 * g + 32, :, :]
                nc.gpsimd.affine_select(out=part, in_=part, compare_op=ALU.not_equal, fill=1.0, base=0,
                                        pattern=[[-1, 2 * NS], [0, P]], channel_multiplier=1)\
                    .then_inc(G("sel"), 1)
            e.wait_ge(G("sel"), 3)
            moe_pool(e, F[0], LNS[0], 0)
            mamba_pool(e)
            e.wait_ge(M("o_psum"), 8)
            expert_numbers()
            moe_pool(e, F[1], LNS[2], 1)
            for s in range(RING):
                e.wait_ge(G(f"scattered{s}"), 2 * 16 * ROUNDS)

        @block.scalar
        def _(e):
            for c in range(HC):
                e.wait_ge(G("biasT"), c + 1)
                nc.scalar.activation(b1T[:, :].rearrange("p (j c a) -> p c a j", a=2, c=HC)[:, c],
                                     ps[:, 4 + c, 0:E].rearrange("p (a j) -> p a j", a=2), ACT.Copy)\
                    .then_inc(G("bias"), 1)
            moe_scalar(e, F[0], LNS[0], 0)
            e.wait_ge(G("mw"), 16 * 9)
            for h in range(C2):
                e.wait_ge(G("vT"), h + 1)
                nc.scalar.activation(vcol[:, h, :], ps[:, 4 + h, 0:8], ACT.Copy).then_inc(G("vcol"), 1)
            nc.scalar.activation(An[:, :, :], An[:, :, :], ACT.Exp).then_inc(G("A"), 1)
            e.wait_ge(G("A"), 1)
            nc.scalar.activation(An[:, :, :], An[:, :, :], ACT.Copy, scale=-1.0).then_inc(G("A"), 1)
            mamba_scalar(e)
            e.wait_ge(G("A"), 2)
            moe_scalar(e, F[1], LNS[2], 1)

        @block.vector
        def _(e):
            moe_vector(e, F[0], LNS[0], 0, lambda i: e.wait_ge(G(f"x{i // 8}"), 16) if i % 8 == 0 else None)
            nc.vector.memset(pad[:, :, :, :, 0:3], 0.0).then_inc(M("pad"), 1)
            e.wait_ge(G("vcol"), C2)
            for h in range(C2):
                nc.vector.tensor_scalar(diagD[:, h, :], ident[:, :], vcol[:, h, 6:7], None, ALU.mult)\
                    .then_inc(M("diagD"), 1)
            e.wait_ge(M("pad"), 1)
            mamba_vector(e)
            moe_vector(e, F[1], LNS[2], 1)

        @block.tensor
        def _(e):
            e.wait_ge(G("ident"), 1)
            e.wait_ge(G("rows"), 16)
            for c in range(HC):
                nc.tensor.transpose(ps[:, 4 + c, 0:E], rows.rearrange("e (p c) -> e c p", c=HC)[:, c, :],
                                    ident[0:E, 0:E]).then_inc(G("biasT"), 1)
            e.wait_ge(G("bias"), HC)
            e.wait_ge(G("gw"), 16)
            moe_tensor(e, F[0], LNS[0], 0)
            e.wait_ge(G("mw"), 16 * 9)
            e.wait_ge(*F[0].at("yo", PAIRS))
            for h in range(C2):
                nc.tensor.transpose(ps[:, 4 + h, 0:8], vrow[:, h * P:(h + 1) * P], ident[0:8, 0:8])\
                    .then_inc(G("vT"), 1)
            e.wait_ge(G("vcol"), C2)
            e.wait_ge(G("sel"), 3)
            mamba_tensor(e)
            moe_tensor(e, F[1], LNS[2], 1)


_INS = ['L0_attn_x', 'L0_attn_W_in', 'L0_attn_conv_w', 'L0_attn_conv_b', 'L0_attn_W_x', 'L0_attn_W_dt',
        'L0_attn_b_dt', 'L0_attn_A_log', 'L0_attn_D', 'L0_attn_W_out', 'L0_ffn_gate_w', 'L0_ffn_gate_b',
        'L0_ffn_w1', 'L0_ffn_b1', 'L0_ffn_w2', 'L0_ffn_b2']
_OUTS = [((BS, SEQ, D), 'float32')]


def kernel(**inputs):
    import numpy as _np
    import concourse.bacc as _bacc
    from concourse.bass_utils import run_bass_kernel_spmd as _run

    nc = _bacc.Bacc("TRN2", target_bir_lowering=False, num_devices=1)
    arrays, args = {}, []
    for name in _INS:
        a = _np.ascontiguousarray(inputs[name])
        arrays[f"in_{name}"] = a
        args.append(nc.dram_tensor(f"in_{name}", a.shape, mybir.dt.from_np(a.dtype), kind="ExternalInput").ap())
    for i, (shape, dtype) in enumerate(_OUTS):
        dt = mybir.dt.from_np(_np.dtype(dtype))
        args.append(nc.dram_tensor(f"out_{i}", shape, dt, kind="ExternalOutput").ap())
    macaron(nc, *args)
    r = _run(nc, [arrays], core_ids=[0])
    return r.results[0]["out_0"]
```

```python
import concourse.bass as bass
from concourse import mybir
from contextlib import ExitStack

FP = mybir.dt.float32
BF = mybir.dt.bfloat16
I32 = mybir.dt.int32
U32 = mybir.dt.uint32
ALU = mybir.AluOpType
ACT = mybir.ActivationFunctionType

P = 128
T = 4096
D = 128
NI = T // P
E = 64
CAP = 64
H = 512
HC = H // P
K = 3
PAIRS = E // 2
RING = 8
ROUNDS = PAIRS // RING
BS, SEQ = 16, 256
C2 = 2
NS = 16
DTR = 64
KC = 4
CH = 512
NQ = T // CH
EPS = 1e-5


PIECES = [(0, 4), (4, 8), (8, 16), (16, 24), (24, 32)]
OUT_PIECES = [(0, 8), (8, 16), (16, 24), (24, 28), (28, 32)]
PIECE = [next(q for q, (i0, i1) in enumerate(PIECES) if i0 <= 4 * g < i1) for g in range(8)]


class Sems:

    def __init__(self, ctx, nc, prefix):
        self._c, self._nc, self._p, self._d = ctx, nc, prefix, {}

    def again(self, use, totals):
        return Use(self, use, totals)

    def __call__(self, name):
        if name not in self._d:
            self._d[name] = self._c.enter_context(self._nc.semaphore(f"{self._p}_{name}"))
        return self._d[name]


class Use:
    def __init__(self, sems, use, totals):
        self._s, self._u, self._t = sems, use, totals

    def __call__(self, name):
        return self._s(name)

    def at(self, name, value):
        return self._s(name), self._u * self._t[name] + value


LN_TOTALS = dict(stats=NI, meanvar=NI, rstd=13, normed=24, normed_act=8, transposed=8, xT=8)
MOE_TOTALS = dict(logits=4, m8=NI, ix8=NI, ixf=1, mdiff=1, gexp=1, gs=3, V=K, marks=2, mask=2, before=1, offset=1,
                  prefix=1, picked=7, WH=K, WL=1, WL_pool=K - 1, place=K, code=1, code_sb=1, slotcode=1, decode=9, xn_stored=16,
                  zeroed=16 * K, x_psum=PAIRS, xt=PAIRS, h_psum=PAIRS, hs=PAIRS, ht_psum=PAIRS, hb=PAIRS,
                  hT=PAIRS, y_psum=PAIRS, yo=PAIRS, gdiag=K * NI // 4 * 3, sum=8, x=8, x4=K * 8)


def macaron(nc, x_in, W_in, conv_w, conv_b, W_x, W_dt, b_dt, A_log, D_w, W_out,
            gate_w, gate_b, w1, b1, w2, b2, out):
    ctx = ExitStack()
    with ctx:
        def sb(name, shape, dt=FP):
            return ctx.enter_context(nc.sbuf_tensor(name, shape, dt))

        xn_dram = [nc.dram_tensor(f"xn_dram{f}", [T, D], FP).ap() for f in range(2)]
        y_dram = [nc.dram_tensor(f"y_dram{f}", [K * T, D], FP).ap() for f in range(2)]

        b2_dram = nc.dram_tensor("b2_dram", [3, E, D], BF).ap()

        X = sb("X", [P, NI, D])
        R1 = sb("R1", [P, 4096])
        R2 = sb("R2", [P, 4096])
        BIG = sb("BIG", [P, 32768])
        ident = sb("ident", [P, P])
        zeros = sb("zeros", [P, 512])
        gw = sb("gw", [P, E])
        gb = sb("gb", [1, E])
        b1T = sb("b1T", [P, PAIRS * HC * 2])
        Win = sb("Win", [P, 2 * C2 * P])
        vrow = sb("vrow", [8, C2 * P])
        vcol = sb("vcol", [P, C2, 8])
        Wx = sb("Wx", [P, C2, DTR + 2 * NS])
        diagD = sb("diagD", [P, C2, P])
        Wdt = sb("Wdt", [DTR, C2 * P])
        Wout = sb("Wout", [P, C2, D])
        An = sb("An", [P, C2, NS])
        sel = sb("sel", [P, 2 * NS], BF)
        state_more = sb("state_more", [P, 2, C2 * CH])
        stack = sb("stack", [P, T], BF)
        st = sb("st", [P, NI, 6])
        mv = sb("mv", [P, NI, 2])
        rstd = sb("rstd", [P, NI])
        rs = sb("rs", [P, 3, NI])
        nmr = sb("nmr", [P, NI])
        gate = sb("gate", [P, NI, K])
        gsum = sb("gsum", [P, NI])
        low = sb("low", [P, K, NI], BF)
        high = sb("high", [P, 1])
        earlier = sb("earlier", [P, P], BF)
        diag_m = sb("diag_m", [P, P], BF)
        ones = sb("ones", [P, E], BF)
        one = sb("one", [1, P])
        ixb = sb("ixb", [P, K, NI], BF)
        ci = sb("ci", [P, PAIRS], I32)
        si = sb("si", [P, PAIRS], I32)
        gtmp = sb("gtmp", [P, 1])
        tok_idx = sb("tok_idx", [P, PAIRS], I32)
        row_idx = sb("row_idx", [P, PAIRS], I32)

        small = stack[:, :].bitcast(FP)
        rows = small[0:E, 0:H]
        m8 = small[:, 640:896].rearrange("p (i k) -> p i k", k=8)
        ix8 = small[:, 896:1152].bitcast(U32).rearrange("p (i k) -> p i k", k=8)

        b2_rows = small[0:E, 1440:1440 + D]
        b2_parts = small[0:E, 1568:1568 + 3 * D // 2].bitcast(BF).rearrange("e (w d) -> e w d", w=3)
        b2_rest = small[0:E, 1760:1760 + D]
        code_sb = small[:, 1152:1152 + CAP]
        rf = small[:, 1280:1280 + 5 * PAIRS].rearrange("p (m j) -> p m j", m=5)

        XN = R1[:, :].rearrange("p (i d) -> p i d", d=D)
        XT = R2[:, :]
        wbuf = [BIG[:, 2048 * s:2048 * s + 2048] for s in range(RING)]
        wbuf += [R1[:, 2048:4096], state_more[:, :, :].rearrange("p u n -> p (u n)")]
        w1s = [w[:, 0:1024].rearrange("p (a h) -> p a h", a=2) for w in wbuf]
        w2s = [w[:, 1024:2048].rearrange("p (a c d) -> p a c d", a=2, c=HC) for w in wbuf]
        B0 = 2048 * RING
        V = R2[:, 0:3072].bitcast(BF).rearrange("p (k e i) -> p k e i", k=K, i=NI)
        mask = R2[:, 3072:4096].bitcast(BF).rearrange("p (e i) -> p e i", i=NI)
        marks = BIG[:, B0:B0 + 1024].bitcast(BF).rearrange("p (e i) -> p e i", i=NI)
        prefix = BIG[:, B0 + 1024:B0 + 2048].bitcast(BF).rearrange("p (e i) -> p e i", i=NI)
        W = BIG[:, B0 + 2048:B0 + 8192].bitcast(BF)\
            .rearrange("p (k w e i) -> p k w e i", k=K, w=2, i=NI)
        B1 = B0 + 8192
        picked = BIG[:, B1:B1 + 3072].bitcast(BF).rearrange("p (k e i) -> p k e i", k=K, i=NI)
        hs = [BIG[:, B1 + 512 * u:B1 + 512 * u + 512] for u in range(2)]
        hb = [BIG[:, B1 + 1024 + 512 * u:B1 + 1536 + 512 * u] for u in range(2)]
        hT = [BIG[:, B1 + 2048 + 512 * u:B1 + 2560 + 512 * u].rearrange("p (c n) -> p c n", c=HC)
              for u in range(2)]
        xt = [BIG[:, B1 + 3072 + 128 * u:B1 + 3200 + 128 * u] for u in range(2)]
        yo = [BIG[:, B1 + 3328 + 128 * s:B1 + 3456 + 128 * s] for s in range(RING)]
        b2s = [BIG[0:3, B1 + 4352 + 128 * s:B1 + 4480 + 128 * s].bitcast(BF).rearrange("w (a d) -> w a d", a=2)
               for s in range(RING)]
        B2 = B1 + 4352 + 128 * RING
        iotaE = BIG[:, B2:B2 + 1024].bitcast(BF).rearrange("p (e i) -> p e i", i=NI)
        place = [BIG[:, c:c + 1024].bitcast(BF).rearrange("p (n i) -> p n i", i=NI)
                 for c in (B0, B0 + 1024, B1 + 3072)]
        assert B2 + 1024 <= 32768
        xg = [R1[:, 128 * s:128 * s + 128] for s in range(RING)]
        gdiag = [R2[:, :], BIG[:, B0:B0 + 4096], BIG[:, B0 + 4096:B0 + 8192]]
        YK = BIG[:, 0:K * 4096].rearrange("p (k i d) -> p k i d", k=K, d=D)
        DT, DTU, HH, SG = [BIG[:, 8192 * m:8192 * m + 8192].rearrange("p (h t) -> p h t", h=C2)
                           for m in range(4)]
        cv = BIG[:, 4200:4200 + 2 * C2 * CH].rearrange("p (u h t) -> p u h t", u=2, h=C2)
        ts = R1[0:DTR, 0:2 * CH].rearrange("p (u t) -> p u t", u=2)
        bcr = R1[32:64, 1024:2048].rearrange("p (u t) -> p u t", u=2)
        dA = R1[:, 0:2048].rearrange("p (u h b t) -> p u h b t", u=2, h=C2, b=2)
        prod = R2[:, 0:2048].rearrange("p (u h t) -> p u h t", u=2, h=C2)
        Cs = R2[:, 2048:3072].rearrange("p (u t) -> p u t", u=2)
        AHEAD = 4
        CRED = 2
        ps = ctx.enter_context(nc.psum_tensor("ps", [P, 8, 512], FP))
        L = ps[:, 0:4, :].rearrange("p g (k e) -> p (g k) e", e=E)
        state = [R1[:, 2048:3072], R1[:, 3072:4096], state_more[:, 0, :], state_more[:, 1, :]]

        G = Sems(ctx, nc, "g")
        M = Sems(ctx, nc, "m")
        moe_sems, ln_sems = Sems(ctx, nc, "e"), Sems(ctx, nc, "l")
        F = [moe_sems.again(n, MOE_TOTALS) for n in range(2)]
        LNS = [ln_sems.again(n, LN_TOTALS) for n in range(3)]

        w1v = w1.rearrange("(a j) d h -> j d a h", a=2)
        b2v = b2_dram.rearrange("w (a j) d -> j w a d", a=2)
        w2v = w2.rearrange("(a j) (p c) d -> j p a (c d)", a=2, c=HC)

        def ln_vector(e, S, before_stats=None):
            for g in range(9):
                for i in range(4 * g, 4 * g + 4) if g < 8 else ():
                    if before_stats:
                        before_stats(i)
                    nc.vector.bn_stats(st[:, i, :], X[:, i, :]).then_inc(S("stats"), 1)
                for i in range(4 * g - 4, 4 * g) if g else ():
                    e.wait_ge(*S.at("stats", i + 1))
                    nc.vector.bn_aggr(mv[:, i, :], st[:, i, :]).then_inc(S("meanvar"), 1)
            n = 0

            def step(instruction):
                nonlocal n
                n += 1
                instruction.then_inc(S("rstd"), 1)
                e.wait_ge(*S.at("rstd", n))

            v, y, z = rs[:, 0, :], rs[:, 1, :], rs[:, 2, :]
            e.wait_ge(*S.at("meanvar", NI))
            step(nc.vector.tensor_scalar(v, mv[:, :, 1], EPS, None, ALU.add))
            step(nc.vector.tensor_single_scalar(z.bitcast(I32), v.bitcast(I32), 1, ALU.arith_shift_right))
            step(nc.vector.tensor_scalar(rstd[:, :].bitcast(I32), z.bitcast(I32), -1.0, float(0x5F3759DF),
                                         ALU.mult, ALU.add))
            for k in range(3):
                step(nc.vector.tensor_tensor(y, rstd[:, :], rstd[:, :], ALU.mult))
                step(nc.vector.scalar_tensor_tensor(out=z, in0=y, scalar=-0.5, in1=v, op0=ALU.mult, op1=ALU.mult))
                step(nc.vector.scalar_tensor_tensor(out=rstd[:, :], in0=z, scalar=1.5, in1=rstd[:, :],
                                                    op0=ALU.add, op1=ALU.mult))
            step(nc.vector.scalar_tensor_tensor(out=nmr[:, :], in0=mv[:, :, 0], scalar=-1.0, in1=rstd[:, :],
                                                op0=ALU.mult, op1=ALU.mult))
            for i in range(NI):
                if i % 4 < 3:
                    nc.vector.tensor_scalar(XN[:, i, :], X[:, i, :], mv[:, i, 0:1], rstd[:, i:i + 1],
                                            ALU.subtract, ALU.mult).then_inc(S("normed"), 1)

        def ln_scalar(e, S):
            e.wait_ge(*S.at("rstd", LN_TOTALS["rstd"]))
            for i in range(3, NI, 4):
                nc.scalar.activation(XN[:, i, :], X[:, i, :], ACT.Identity, bias=nmr[:, i:i + 1],
                                     scale=rstd[:, i:i + 1]).then_inc(S("normed_act"), 1)

        def ln_transpose(e, S, g):
            e.wait_ge(*S.at("normed", 3 * g + 3))
            e.wait_ge(*S.at("normed_act", g + 1))
            if g >= 4:
                e.wait_ge(*S.at("xT", g - 3))
            for k in range(4):
                last = nc.tensor.transpose(ps[:, 4 + g % 4, k * P:(k + 1) * P], XN[:, 4 * g + k, :], ident[:, :])
            last.then_inc(S("transposed"), 1)

        def ln_copy(e, S, g, in_time_order):
            e.wait_ge(*S.at("transposed", g + 1))
            src = ps[:, 4 + g % 4, :].rearrange("d (k p) -> d k p", k=4)
            if in_time_order:
                dst = XT.rearrange("d (p i) -> d i p", i=NI)[:, 4 * g:4 * g + 4, :]
            else:
                dst = XT.rearrange("d (i p) -> d i p", i=NI)[:, 4 * g:4 * g + 4, :]
            nc.scalar.activation(dst, src, ACT.Copy).then_inc(S("xT"), 1)

        EARLY = (2, 3)

        def weights(name, f, r, s):
            if type(r) is int and r == ROUNDS - 1 and s in EARLY:
                b = RING + EARLY.index(s)
                return b, G(f"{name}_{b}"), 16 * (f + 1)
            loads = ROUNDS - (s in EARLY)
            return s, G(f"{name}_{s}"), 16 * (loads * f + r + 1)

        def moe_sync(e, S, f):
            def load_w1(r, s):
                b, loaded, _ = weights("w1", f, r, s)
                e.dma_start(w1s[b], w1v[bass.ds(RING * r + s, 1)].rearrange("o d a h -> (o d) a h"))\
                    .then_inc(loaded, 16)

            def load_w2(r, s):
                b, loaded, _ = weights("w2", f, r, s)
                e.dma_start(wbuf[b][:, 1024:2048].rearrange("p (a h) -> p a h", a=2),
                            w2v[bass.ds(RING * r + s, 1)].rearrange("o p a h -> (o p) a h")).then_inc(loaded, 16)

            def load_b2(r, s):
                e.dma_start(b2s[s], b2v[bass.ds(RING * r + s, 1)].rearrange("o w a d -> (o w) a d")).then_inc(G(f"b2_{s}"), 16)

            def reload_w1(j, s, r):
                if not (type(r) is int and r == ROUNDS - 1 and s in EARLY):
                    e.wait_ge(*S.at("h_psum", j - RING + 1))
                    load_w1(r, s)

            def reload_w2(j, s, r):
                e.wait_ge(*S.at("y_psum", j - RING + 1))
                load_b2(r, s)
                if not (type(r) is int and r == ROUNDS - 1 and s in EARLY):
                    load_w2(r, s)

            for s in range(RING):
                load_w1(0, s)
                load_w2(0, s)
            if f == 0:
                e.wait_ge(G("b2_stored"), 16)
            for s in range(RING):
                load_b2(0, s)
            last = ROUNDS - 1
            load_w1(last, EARLY[1])
            load_w2(last, EARLY[1])
            e.wait_ge(*S.at("xn_stored", 16))
            e.wait_ge(*LNS[2 * f].at("transposed", 8))
            load_w1(last, EARLY[0])
            load_w2(last, EARLY[0])
            if f == 0:
                for k in range(K):
                    e.dma_start(y_dram[0][k * T:(k + 1) * T, :].rearrange("(p a i) d -> p a (i d)", p=P, a=8),
                                zeros[:, :].unsqueeze(1).broadcast_to([P, 8, 512])).then_inc(S("zeroed"), 16)
            for s in range(2):
                reload_w1(RING + s, s, 1)
            pipeline(e, RING, ROUNDS, [(2, reload_w1), (0, reload_w2)], 1)
            e.wait_ge(*S.at("y_psum", PAIRS))
            for s in range(RING):
                e.wait_ge(G(f"scattered{s}"), 16 * ROUNDS * (f + 1))
            yv = y_dram[f].rearrange("(k p i) d -> k p i d", k=K, p=P)
            for q, (i0, i1) in enumerate(PIECES):
                for k in range(K):
                    e.dma_start(YK[:, k, i0:i1, :], yv[k, :, i0:i1, :]).then_inc(G(f"yk{q}"), 16)

        def moe_scalar(e, S, LS, f):
            ln_scalar(e, LS)
            for g in range(8):
                ln_copy(e, LS, g, False)
            if f == 0:
                e.wait_ge(G("code"), 5)
            for k in range(K):
                e.wait_ge(*S.at("V", k + 1))
                nc.scalar.activation(W[:, k, 0], V[:, k], ACT.Copy, scale=high[:, 0:1]).then_inc(S("WH"), 1)
            e.wait_ge(*S.at("mdiff", 1))
            nc.scalar.activation(gate[:, :, :], gate[:, :, :], ACT.Exp).then_inc(S("gexp"), 1)

            def xt_copy(j, s, r):
                e.wait_ge(*S.at("x_psum", j + 1))
                if not (type(j) is int and j < 2):
                    e.wait_ge(*S.at("h_psum", j - 1))
                nc.scalar.activation(xt[s % 2], ps[:, 7 * (s % 2), 0:P], ACT.Copy).then_inc(S("xt"), 1)

            def gelu(j, s, r):
                e.wait_ge(*S.at("hb", j + 1))
                if not (type(j) is int and j < 2):
                    e.wait_ge(*S.at("y_psum", j - 1))
                nc.scalar.activation(hT[s % 2].rearrange("p c n -> p (c n)"), hb[s % 2], ACT.Gelu)\
                    .then_inc(S("hT"), 1)

            def gate_diagonals(j, s, r):
                if s % 4 == 3:
                    return
                for k in range(K):
                    nc.scalar.activation(gdiag[k][:, bass.ds(P * j, P)], ident[:, :], ACT.Copy,
                                         scale=gate[:, bass.ds(j, 1), k]).then_inc(S("gdiag"), 1)

            nc.scalar.activation(gtmp[:, :], ident[:, 0:1], ACT.Gelu)
            for j in range(3):
                xt_copy(j, j, 0)
            e.wait_ge(*S.at("gs", 3))
            gelu(0, 0, 0)
            pipeline(e, RING, ROUNDS, [(3, xt_copy), (1, gelu), (0, gate_diagonals)])

        def pipeline(e, ring, rounds, stages, start=0):
            def one(r):
                for s in range(ring):
                    for lead, do in stages:
                        j, slot, rr = ring * r + s + lead, (s + lead) % ring, r + (s + lead) // ring
                        if type(r) is int and not 0 <= j < ring * rounds:
                            continue
                        do(j, slot, rr)
            one(start)
            with e.Fori(start + 1, rounds - 1) as r:
                one(r)
            one(rounds - 1)

        def moe_tensor(e, S, LS, f):
            def logits(g):
                e.wait_ge(*LS.at("xT", 2 * g + 2))
                for k in range(8):
                    i = 8 * g + k
                    last = nc.tensor.matmul(ps[:, g, E * k:E * k + E], XT[:, i * P:i * P + P], gw[:, :],
                                            start=False, stop=(k == 7))
                last.then_inc(S("logits"), 1)

            if f == 0:
                e.wait_ge(G("one"), 1)
            else:
                e.wait_ge(M("x"), 8)
            for g in range(4):
                nc.tensor.matmul(ps[:, g, :], one[:, :], gb[:, :].unsqueeze(1).broadcast_to([1, 8, E]),
                                 start=True, stop=False)
            for g in range(8):
                ln_transpose(e, LS, g)
                if g >= 3 and g % 2 == 1:
                    logits((g - 3) // 2)
            logits(3)
            e.wait_ge(*S.at("marks", 2))
            if f == 0:
                e.wait_ge(G("code"), 5)
            for i in range(NI):
                nc.tensor.matmul(ps[:, 4, 0:E], earlier[:, :], marks[:, :, i], start=(i == 0), stop=False)
            nc.tensor.matmul(ps[:, 4, 0:E], diag_m[:, :], ones[:, :], start=False, stop=True).then_inc(S("before"), 1)
            e.wait_ge(*S.at("WL", 1))
            for k in range(K):
                e.wait_ge(*S.at("WH", k + 1))
                if k:
                    e.wait_ge(*S.at("WL_pool", k))
                e.wait_ge(*S.at("place", k + 1))
                for i in range(NI):
                    last = nc.tensor.matmul(ps[:, 5, 0:CAP], W[:, k].rearrange("p w e i -> p i (w e)")[:, i, :],
                                            place[k][:, :, i], start=(k == 0 and i == 0),
                                            stop=(k == K - 1 and i == NI - 1))
            last.then_inc(S("code"), 1)
            e.wait_ge(*S.at("code_sb", 1))
            for a in range(2):
                last = nc.tensor.matmul(ps[a * CAP:(a + 1) * CAP, 6, 0:2 * PAIRS], code_sb[:, :],
                                        ident[:, :].rearrange("p (w a j) -> p a w j", w=2, a=2)[:, a],
                                        start=True, stop=True)
            last.then_inc(S("slotcode"), 1)

            def later(j):
                return not (type(j) is int and j < 2)

            def t_in(j, s, r):
                e.wait_ge(G(f"gathered{s}"), 16 * (ROUNDS * f + r + 1))
                if later(j):
                    e.wait_ge(*S.at("xt", j - 1))
                nc.tensor.transpose(ps[:, 7 * (s % 2), 0:P], xg[s], ident[:, :]).then_inc(S("x_psum"), 1)

            def mm1(j, s, r):
                e.wait_ge(*S.at("xt", j + 1))
                b, loaded, count = weights("w1", f, r, s)
                e.wait_ge(loaded, count)
                if later(j):
                    e.wait_ge(*S.at("hs", j - 1))
                for a in range(2):
                    last = nc.tensor.matmul(ps[a * CAP:(a + 1) * CAP, 1 + s % 2, :], xt[s % 2][:, a * CAP:(a + 1) * CAP],
                                            w1s[b][:, a, :], start=True, stop=True)
                last.then_inc(S("h_psum"), 1)

            def ht(j, s, r):
                e.wait_ge(*S.at("hs", j + 1))
                if later(j):
                    e.wait_ge(*S.at("hb", j - 1))
                for c in range(HC):
                    last = nc.tensor.transpose(ps[:, 3 + s % 2, c * P:(c + 1) * P],
                                               hs[s % 2].rearrange("n (p c) -> n c p", c=HC)[:, c, :], ident[:, :])
                last.then_inc(S("ht_psum"), 1)

            def mm2(j, s, r):
                e.wait_ge(*S.at("hT", j + 1))
                b, loaded, count = weights("w2", f, r, s)
                e.wait_ge(loaded, count)
                if later(j):
                    e.wait_ge(*S.at("yo", j - 1))
                e.wait_ge(G(f"b2_{s}"), 16 * (ROUNDS * f + r + 1))
                for a in range(2):
                    nc.tensor.matmul(ps[a * CAP:(a + 1) * CAP, 5 + s % 2, 0:D], ones[0:3, 0:CAP], b2s[s][:, a, :],
                                     start=True, stop=False)
                for c in range(HC):
                    for a in range(2):
                        last = nc.tensor.matmul(ps[a * CAP:(a + 1) * CAP, 5 + s % 2, 0:D],
                                                hT[s % 2][:, c, a * CAP:(a + 1) * CAP], w2s[b][:, a, c, :],
                                                start=False, stop=(c == HC - 1))
                last.then_inc(S("y_psum"), 1)

            t_in(0, 0, 0)
            t_in(1, 1, 0)
            mm1(0, 0, 0)
            t_in(2, 2, 0)
            mm1(1, 1, 0)
            ht(0, 0, 0)
            pipeline(e, RING, ROUNDS, [(3, t_in), (2, mm1), (1, ht), (0, mm2)])
            e.wait_ge(*S.at("gdiag", MOE_TOTALS["gdiag"]))
            e.wait_ge(*S.at("yo", PAIRS))
            for g in range(8):
                e.wait_ge(G(f"yk{PIECE[g]}"), 16 * K * (f + 1))
                for i in range(4 * g, 4 * g + 3):
                    for k in range(K):
                        last = nc.tensor.matmul(ps[:, g, (i % 4) * P:(i % 4 + 1) * P],
                                                gdiag[k][:, P * i:P * i + P], YK[:, k, i, :],
                                                start=(k == 0), stop=(k == K - 1))
                last.then_inc(S("sum"), 1)

        def moe_vector(e, S, LS, f, before_stats=None):
            ln_vector(e, LS, before_stats)
            for g in range(5):
                for i in range(8 * g - 8, 8 * g) if g else ():
                    e.wait_ge(*S.at("m8", i + 1))
                    nc.vector.max_index(ix8[:, i, :], m8[:, i, :], L[:, i, :]).then_inc(S("ix8"), 1)
                for i in range(8 * g, 8 * g + 8) if g < 4 else ():
                    e.wait_ge(*S.at("logits", g + 1))
                    nc.vector.max(m8[:, i, :], L[:, i, :]).then_inc(S("m8"), 1)
            e.wait_ge(*S.at("ix8", NI))
            nc.vector.tensor_copy(ixb[:, :, :].rearrange("p k i -> p i k"), ix8[:, :, 0:K]).then_inc(S("ixf"), 1)
            nc.vector.tensor_tensor(gate[:, :, :], m8[:, :, 0:K], m8[:, :, 0:1].broadcast_to([P, NI, K]),
                                    ALU.subtract).then_inc(S("mdiff"), 1)
            e.wait_ge(*S.at("ixf", 1))
            e.wait_ge(G("code"), 5 + f)
            for k in range(K):
                nc.vector.tensor_tensor(V[:, k], iotaE, ixb[:, k, :].unsqueeze(1).broadcast_to([P, E, NI]),
                                        ALU.is_equal).then_inc(S("V"), 1)
            for k in range(1, K):
                e.wait_ge(*S.at("V", k + 1))
                if k > 1:
                    e.wait_ge(*S.at("marks", k - 1))
                nc.vector.tensor_tensor(marks, V[:, 0] if k == 1 else marks, V[:, k], ALU.add)\
                    .then_inc(S("marks"), 1)
            nc.vector.tensor_tensor(W[:, 0, 1], V[:, 0], low[:, 0, :].unsqueeze(1).broadcast_to([P, E, NI]),
                                    ALU.mult).then_inc(S("WL"), 1)
            e.wait_ge(*S.at("before", 1))
            nc.vector.scalar_tensor_tensor(out=marks[:, :, 0], in0=ps[:, 4, 0:E], scalar=float(2 * CAP),
                                           in1=marks[:, :, 0], op0=ALU.min, op1=ALU.add).then_inc(S("offset"), 1)
            e.wait_ge(*S.at("offset", 1))
            e.wait_ge(*S.at("mask", 2))
            nc.vector.tensor_tensor_scan(prefix.rearrange("p e i -> p (e i)"), mask.rearrange("p e i -> p (e i)"),
                                         marks.rearrange("p e i -> p (e i)"), 0.0, ALU.mult, ALU.add)\
                .then_inc(S("prefix"), 1)
            e.wait_ge(*S.at("prefix", 1))
            nc.vector.tensor_tensor(picked, V, prefix.unsqueeze(1).broadcast_to([P, K, E, NI]), ALU.mult)\
                .then_inc(S("picked"), 1)
            half = E // 2
            for n in range(6):
                e.wait_ge(*S.at("picked", n + 1))
                nc.vector.tensor_tensor(picked[:, :, 0:half], picked[:, :, 0:half], picked[:, :, half:2 * half],
                                        ALU.add).then_inc(S("picked"), 1)
                half //= 2
            e.wait_ge(*S.at("picked", 7))
            for k in range(K):
                nc.vector.tensor_tensor(place[k], iotaE, picked[:, k, 0:1, :].broadcast_to([P, CAP, NI]),
                                        ALU.is_equal).then_inc(S("place"), 1)
            e.wait_ge(*S.at("gexp", 1))
            nc.vector.reduce_sum(gsum[:, :], gate[:, :, :], axis=mybir.AxisListType.X).then_inc(S("gs"), 1)
            e.wait_ge(*S.at("gs", 1))
            nc.vector.reciprocal(gsum[:, :], gsum[:, :]).then_inc(S("gs"), 1)
            e.wait_ge(*S.at("gs", 2))
            nc.vector.scalar_tensor_tensor(out=gate[:, :, :], in0=gate[:, :, :], scalar=0.5,
                                           in1=gsum[:, :].unsqueeze(2).broadcast_to([P, NI, K]),
                                           op0=ALU.mult, op1=ALU.mult).then_inc(S("gs"), 1)
            n = 0

            def dec(instruction):
                nonlocal n
                n += 1
                instruction.then_inc(S("decode"), 1)
                e.wait_ge(*S.at("decode", n))

            high_part, low_part = ps[:, 6, 0:PAIRS], ps[:, 6, PAIRS:2 * PAIRS]
            base, tok, k32, row, empty = [rf[:, m, :] for m in range(5)]
            e.wait_ge(*S.at("code", 1))
            nc.vector.tensor_copy(code_sb[:, :], ps[:, 5, 0:CAP]).then_inc(S("code_sb"), 1)
            e.wait_ge(*S.at("slotcode", 1))
            dec(nc.vector.tensor_copy(ci[:, :], low_part))
            nc.vector.tensor_single_scalar(si[:, :], ci[:, :], NI - 1, ALU.bitwise_and).then_inc(S("decode"), 1)
            nc.vector.tensor_scalar(base, high_part, float(NI), float(-NI), ALU.mult, ALU.add).then_inc(S("decode"), 1)
            e.wait_ge(*S.at("decode", 3))
            nc.vector.tensor_tensor(tok, base, si[:, :], ALU.add).then_inc(S("decode"), 1)
            nc.vector.tensor_tensor(k32, low_part, si[:, :], ALU.subtract).then_inc(S("decode"), 1)
            e.wait_ge(*S.at("decode", 4))
            nc.vector.tensor_scalar(tok_idx[:, :], tok, 0.0, None, ALU.max).then_inc(S("decode"), 1)
            nc.vector.tensor_scalar(empty, high_part, 0.0, float(2 * K * T), ALU.is_equal, ALU.mult)\
                .then_inc(S("decode"), 1)
            e.wait_ge(*S.at("decode", 5))
            nc.vector.scalar_tensor_tensor(out=row, in0=k32, scalar=float(T // NI), in1=tok,
                                           op0=ALU.mult, op1=ALU.add).then_inc(S("decode"), 1)
            e.wait_ge(*S.at("decode", 8))
            nc.vector.tensor_tensor(row_idx[:, :], row, empty, ALU.add).then_inc(S("decode"), 1)

            def later(j):
                return not (type(j) is int and j < 2)

            def h_copy(j, s, r):
                e.wait_ge(*S.at("h_psum", j + 1))
                if later(j):
                    e.wait_ge(*S.at("ht_psum", j - 1))
                nc.vector.tensor_copy(hs[s % 2], ps[:, 1 + s % 2, :]).then_inc(S("hs"), 1)

            def bias1(j, s, r):
                e.wait_ge(*S.at("ht_psum", j + 1))
                if later(j):
                    e.wait_ge(*S.at("hT", j - 1))
                bias = b1T[:, bass.ds(2 * HC * j, 2 * HC)].unsqueeze(2).broadcast_to([P, 2 * HC, CAP])
                nc.vector.tensor_tensor(hb[s % 2].rearrange("p (c n) -> p c n", n=CAP),
                                        ps[:, 3 + s % 2, :].rearrange("p (c n) -> p c n", n=CAP), bias,
                                        ALU.add).then_inc(S("hb"), 1)

            def y_copy(j, s, r):
                e.wait_ge(*S.at("y_psum", j + 1))
                if f or not (type(r) is int and r == 0):
                    e.wait_ge(G(f"scattered{s}"), 16 * (ROUNDS * f + r))
                nc.vector.tensor_copy(yo[s], ps[:, 5 + s % 2, 0:D]).then_inc(S("yo"), 1)

            h_copy(0, 0, 0)
            h_copy(1, 1, 0)
            bias1(0, 0, 0)
            pipeline(e, RING, ROUNDS, [(2, h_copy), (1, bias1), (0, y_copy)])

        def moe_residual(e, S, f, g):
            i = 4 * g + 3
            e.wait_ge(G(f"yk{PIECE[g]}"), 16 * K * (f + 1))
            for k in range(K):
                if k:
                    e.wait_ge(*S.at("x4", K * g + k))
                nc.vector.scalar_tensor_tensor(out=X[:, i, :], in0=YK[:, k, i, :], scalar=gate[:, i, k:k + 1],
                                               in1=X[:, i, :], op0=ALU.mult, op1=ALU.add).then_inc(S("x4"), 1)
                if k == 0:
                    e.wait_ge(*S.at("sum", g + 1))
                    t = X[:, 4 * g:4 * g + 3, :].rearrange("p i d -> p (i d)")
                    nc.vector.tensor_tensor(t, t, ps[:, g, 0:3 * D], ALU.add).then_inc(S("x"), 1)

        def moe_residual_ahead(e, S, i):
            if i % 4 == 0:
                if i == 0:
                    moe_residual(e, S, 0, 0)
                if i + 4 < NI:
                    moe_residual(e, S, 0, i // 4 + 1)
                e.wait_ge(*S.at("x", i // 4 + 1))
                e.wait_ge(*S.at("x4", K * (i // 4 + 1)))

        def moe_pool(e, S, LS, f):
            e.wait_ge(*LS.at("normed", 24))
            e.wait_ge(*LS.at("normed_act", 8))
            e.dma_start(xn_dram[f].rearrange("(p i) d -> p (i d)", p=P), R1[:, :]).then_inc(S("xn_stored"), 16)
            e.wait_ge(*S.at("logits", 4))
            nc.gpsimd.memset(mask, 1.0).then_inc(S("mask"), 1)
            e.wait_ge(*S.at("mask", 1))
            nc.gpsimd.memset(mask[:, :, 0:1], 0.0).then_inc(S("mask"), 1)
            for k in range(1, K):
                e.wait_ge(*S.at("V", k + 1))
                nc.gpsimd.tensor_tensor(W[:, k, 1], V[:, k], low[:, k, :].unsqueeze(1).broadcast_to([P, E, NI]),
                                        ALU.mult).then_inc(S("WL_pool"), 1)
            e.wait_ge(*S.at("xn_stored", 16))
            e.wait_ge(*S.at("decode", 6))

            def gather(j):
                s = j % RING
                if j >= RING:
                    e.wait_ge(*S.at("x_psum", j - RING + 1))
                nc.gpsimd.indirect_dma_start(
                    xg[s], None, xn_dram[f], bass.IndirectOffsetOnAxis(tok_idx[:, j:j + 1].bitcast(U32), 0),
                    bounds_check=T - 1, oob_is_err=False).then_inc(G(f"gathered{s}"), 16)

            for j in range(RING):
                gather(j)
            e.wait_ge(*S.at("decode", 9))
            if f == 0:
                e.wait_ge(*S.at("zeroed", 16 * K))
            else:
                e.wait_ge(M("zeroed"), 16 * K)
            for j in range(PAIRS):
                s = j % RING
                e.wait_ge(*S.at("yo", j + 1))
                nc.gpsimd.indirect_dma_start(
                    y_dram[f], bass.IndirectOffsetOnAxis(row_idx[:, j:j + 1].bitcast(U32), 0), yo[s], None,
                    bounds_check=K * T - 1, oob_is_err=False).then_inc(G(f"scattered{s}"), 16)
                if j + RING < PAIRS:
                    gather(j + RING)

        def mamba_tensor(e):
            LS = LNS[1]
            e.wait_ge(*F[0].at("x", 8))
            for g in range(8):
                ln_transpose(e, LS, g)
            e.wait_ge(*LS.at("xT", 8))

            def raw(q, u, r):
                e.wait_ge(M("conv"), 2 * (q - 2 + CRED) + 2)
                for m in range(2):
                    last = nc.tensor.matmul(ps[:, 2 * u + m, :], Win[:, m * P:(m + 1) * P],
                                            XT[:, bass.ds(CH * q, CH)], start=True, stop=True)
                last.then_inc(M("raw_psum"), 1)

            def gates(q, u, r):
                e.wait_ge(M("sg"), q - 2 + CRED + 1)
                for m in range(2):
                    last = nc.tensor.matmul(ps[:, 4 + 2 * u + m, :], Win[:, (2 + m) * P:(3 + m) * P],
                                            XT[:, bass.ds(CH * q, CH)], start=True, stop=True)
                last.then_inc(M("gate_psum"), 1)

            pipeline(e, 2, NQ // 2, [(0, raw), (0, gates)])

            def x_proj(q, u, r):
                e.wait_ge(M("h"), q + 1 + CRED)
                e.wait_ge(M("ts"), q - 2 + CRED + 1)
                e.wait_ge(M("rest"), q - 2 + CRED + 1)
                for h in range(C2):
                    last = nc.tensor.matmul(ps[0:DTR + 2 * NS, u, :], Wx[:, h, :], HH[:, h, bass.ds(CH * q, CH)],
                                            start=(h == 0), stop=(h == C2 - 1))
                last.then_inc(M("x_psum"), 1)

            def dt_proj(q, u, r):
                e.wait_ge(M("ts"), q + 1 + CRED)
                e.wait_ge(M("z"), q - 2 + CRED + 1)
                for h in range(C2):
                    last = nc.tensor.matmul(ps[:, 2 + 2 * u + h, :], Wdt[:, h * P:(h + 1) * P], ts[:, u, :],
                                            start=True, stop=True)
                last.then_inc(M("dt_psum"), 1)

            e.wait_ge(M("conv"), 2 * (NQ - 1 + CRED))
            x_proj(0, 0, 0)
            x_proj(1, 1, 0)
            e.wait_ge(M("conv"), 2 * (NQ + CRED))
            e.wait_ge(M("sg"), NQ + CRED)
            pipeline(e, 2, NQ // 2, [(0, dt_proj), (2, x_proj)])

            e.wait_ge(M("z"), NQ + CRED)
            e.wait_ge(M("stack"), NQ + CRED)
            e.wait_ge(M("diagD"), C2)

            def spread_b(q, n):
                step = NS * q + n
                e.wait_ge(M("dbu"), step - 2 + CRED + 1)
                nc.tensor.matmul(ps[:, 2 * (n % 2), :], sel[0:96, n:n + 1].broadcast_to([96, P]), stack[0:96, bass.ds(CH * q, CH)],
                                 start=True, stop=True).then_inc(M("b_psum"), 1)

            def spread_c(q, n):
                step = NS * q + n
                e.wait_ge(M("cs"), step - 2 + CRED + 1)
                nc.tensor.matmul(ps[:, 1 + 2 * (n % 2), :], sel[0:96, NS + n:NS + n + 1].broadcast_to([96, P]), stack[0:96, bass.ds(CH * q, CH)],
                                 start=True, stop=True).then_inc(M("c_psum"), 1)

            def chunk(q, u, last_chunk):
                for n in range(NS):
                    for ahead, spread in ((3, spread_c), (4, spread_b)):
                        if n + ahead < NS:
                            spread(q, n + ahead)
                        elif not last_chunk:
                            spread(q + 1, n + ahead - NS)
                    if n == 0:
                        e.wait_ge(M("y"), q - 2 + CRED + 1)
                        for h in range(C2):
                            nc.tensor.matmul(ps[:, 4 + 2 * u + h, :], diagD[:, h, :], HH[:, h, bass.ds(CH * q, CH)],
                                             start=True, stop=False)
                    e.wait_ge(M("prod"), NS * q + n + 1 + AHEAD)
                    for h in range(C2):
                        last = nc.tensor.matmul(ps[:, 4 + 2 * u + h, :], ident[:, :], prod[:, n % 2, h, :],
                                                start=False, stop=(n == NS - 1))
                    last.then_inc(M("summed"), 1)

            for n in range(4):
                spread_b(0, n)
                if n < 3:
                    spread_c(0, n)
            with e.Fori(0, NQ // 2 - 1) as r:
                for u in range(2):
                    chunk(2 * r + u, u, False)
            for u in range(2):
                chunk(NQ - 2 + u, u, u == 1)

            e.wait_ge(M("y"), NQ + CRED)
            for g in range(8):
                if g >= 2:
                    e.wait_ge(M("x"), g - 1)
                for k in range(4):
                    for h in range(C2):
                        lhsT = SG[:, h, :].rearrange("p (q i) -> p i q", i=NI)[:, 4 * g + k, :]
                        last = nc.tensor.matmul(ps[:, g % 2, k * P:(k + 1) * P], lhsT, Wout[:, h, :],
                                                start=(h == 0), stop=(h == C2 - 1))
                last.then_inc(M("o_psum"), 1)

        def mamba_scalar(e):
            LS = LNS[1]

            def own_wait():
                e.sem_inc(M("held"), 1)

            ln_scalar(e, LS)
            for g in range(8):
                ln_copy(e, LS, g, True)

            def last_tap(q, u, r):
                e.wait_ge(M("raw_psum"), q + 1)
                e.wait_ge(M("h"), q - 2 + CRED + 1)
                for h in range(C2):
                    last = nc.scalar.activation(cv[:, u, h, :], ps[:, 2 * u + h, :], ACT.Identity,
                                                bias=vcol[:, h, 4:5], scale=vcol[:, h, 3:4])
                last.then_inc(M("last_tap"), 1)

            def gate_silu(q, u, r):
                e.wait_ge(M("gate_psum"), q + 1)
                own_wait()
                nc.scalar.activation(SG[:, :, bass.ds(CH * q, CH)], ps[:, 4 + 2 * u:6 + 2 * u, :], ACT.Silu)\
                    .then_inc(M("sg"), 1)

            def h_silu(q, u, r):
                e.wait_ge(M("conv"), 2 * (q + 1 + CRED))
                own_wait()
                nc.scalar.activation(HH[:, :, bass.ds(CH * q, CH)], cv[:, u, :, :], ACT.Silu).then_inc(M("h"), 1)

            last_tap(0, 0, 0)
            pipeline(e, 2, NQ // 2, [(-1, h_silu), (1, last_tap), (0, gate_silu)])
            h_silu(NQ - 1, 1, NQ // 2 - 1)

            def x_parts(q, u, r):
                e.wait_ge(M("x_psum"), q + 1)
                e.wait_ge(M("dt_psum"), q - 2 + CRED + 1)
                nc.scalar.activation(ts[:, u, :], ps[0:DTR, u, :], ACT.Copy).then_inc(M("ts"), 1)
                nc.scalar.activation(stack[0:32, bass.ds(CH * q, CH)], ps[DTR:DTR + 2 * NS, u, :], ACT.Copy)\
                    .then_inc(M("hi"), 1)

            def mid(q, u, r):
                e.wait_ge(M("rest"), q + 1 + CRED)
                own_wait()
                nc.scalar.activation(stack[32:64, bass.ds(CH * q, CH)], bcr[:, u, :], ACT.Copy).then_inc(M("mid"), 1)

            def exponential(q, u, r):
                e.wait_ge(M("minus_abs"), q + 1)
                own_wait()
                t = DTU[:, :, bass.ds(CH * q, CH)]
                nc.scalar.activation(t, t, ACT.Exp).then_inc(M("exp"), 1)

            x_parts(0, 0, 0)
            mid(0, 0, 0)
            x_parts(1, 1, 0)
            pipeline(e, 2, NQ // 2, [(2, x_parts), (0, exponential), (1, mid)])
            e.wait_ge(M("exp"), NQ)
            for q in range(NQ):
                t = DTU[:, :, CH * q:CH * q + CH]
                nc.scalar.activation(t, t, ACT.Ln, bias=1.0).then_inc(M("ln"), 1)

            e.wait_ge(M("stack"), NQ + CRED)
            e.wait_ge(M("dA_zero"), 1)
            with e.Fori(0, NQ) as q:
                for n in range(NS):
                    step = NS * q + n
                    if n == 0:
                        e.wait_ge(M("dt"), q + 1)
                    e.wait_ge(M("scanned"), step - 2 + AHEAD + 1)
                    own_wait()
                    for h in range(C2):
                        nc.scalar.activation(
                            dA[:, n % 2, h, :, 1:SEQ],
                            DT[:, h, bass.ds(CH * q, CH)].rearrange("p (b t) -> p b t", b=2)[:, :, 1:SEQ],
                            ACT.Exp, scale=An[:, h, n:n + 1]).then_inc(M("dA"), 1)
                    e.wait_ge(M("c_psum"), step + 1)
                    e.wait_ge(M("prod"), step - 2 + AHEAD + 1)
                    nc.scalar.activation(Cs[:, n % 2, :], ps[:, 1 + 2 * (n % 2), :], ACT.Copy).then_inc(M("cs"), 1)

        def mamba_vector(e):
            ln_vector(e, LNS[1], lambda i: moe_residual_ahead(e, F[0], i))

            def conv(q, u, r):
                e.wait_ge(M("last_tap"), q + 1)
                for k in range(KC - 1):
                    back = KC - 1 - k
                    for h in range(C2):
                        o = cv[:, u, h, :].rearrange("p (b t) -> p b t", b=2)[:, :, back:]
                        row = ps[:, 2 * u + h, :].rearrange("p (b t) -> p b t", b=2)[:, :, 0:SEQ - back]
                        if k:
                            e.wait_ge(M("tap"), 2 * C2 * q + C2 * (k - 1) + h + 1)
                        nc.vector.scalar_tensor_tensor(out=o, in0=row, scalar=vcol[:, h, k:k + 1], in1=o,
                                                       op0=ALU.mult, op1=ALU.add)\
                            .then_inc(M("tap" if k < KC - 2 else "conv"), 1)

            pipeline(e, 2, NQ // 2, [(0, conv)])

            def rest(q, u, r):
                e.wait_ge(M("hi"), q + 1)
                e.wait_ge(M("stack"), q - 2 + CRED + 1)
                nc.vector.tensor_tensor(bcr[:, u, :], ps[DTR:DTR + 2 * NS, u, :], stack[0:32, bass.ds(CH * q, CH)],
                                        ALU.subtract).then_inc(M("rest"), 1)

            def z(q, u, r):
                e.wait_ge(M("dt_psum"), q + 1 + CRED)
                for h in range(C2):
                    last = nc.vector.tensor_scalar(DT[:, h, bass.ds(CH * q, CH)], ps[:, 2 + 2 * u + h, :],
                                                   vcol[:, h, 5:6], None, ALU.add)
                last.then_inc(M("z"), 1)

            def minus_abs(q, u, r):
                e.wait_ge(M("z"), q + 1 + CRED)
                t = DT[:, :, bass.ds(CH * q, CH)]
                nc.vector.scalar_tensor_tensor(out=DTU[:, :, bass.ds(CH * q, CH)], in0=t, scalar=-1.0, in1=t,
                                               op0=ALU.mult, op1=ALU.min).then_inc(M("minus_abs"), 1)

            e.wait_ge(M("h"), NQ + CRED)
            rest(0, 0, 0)
            z(0, 0, 0)
            rest(1, 1, 0)
            pipeline(e, 2, NQ // 2, [(0, minus_abs), (2, rest), (1, z)])

            def dt(q):
                e.wait_ge(M("ln"), q + 1)
                t = DT[:, :, bass.ds(CH * q, CH)]
                nc.vector.scalar_tensor_tensor(out=t, in0=t, scalar=0.0, in1=DTU[:, :, bass.ds(CH * q, CH)],
                                               op0=ALU.max, op1=ALU.add).then_inc(M("dt"), 1)

            def dtu(q):
                e.wait_ge(M("dt"), q + 1)
                nc.vector.tensor_tensor(DTU[:, :, bass.ds(CH * q, CH)], DT[:, :, bass.ds(CH * q, CH)],
                                        HH[:, :, bass.ds(CH * q, CH)], ALU.mult).then_inc(M("dtu"), 1)

            def y_out(q, u):
                e.wait_ge(M("summed"), NS * q + NS + CRED)
                t = SG[:, :, bass.ds(CH * q, CH)]
                nc.vector.tensor_tensor(t, ps[:, 4 + 2 * u:6 + 2 * u, :], t, ALU.mult).then_inc(M("y"), 1)

            def times_b(q, n):
                step = NS * q + n
                if n == 0:
                    e.wait_ge(M("dtu"), q + 1)
                e.wait_ge(M("b_psum"), step + 1)
                e.wait_ge(M("prod"), step - AHEAD + AHEAD + 1)
                nc.vector.tensor_tensor(state[n % AHEAD].rearrange("p (h t) -> p h t", h=C2),
                                        DTU[:, :, bass.ds(CH * q, CH)],
                                        ps[:, 2 * (n % 2), :].unsqueeze(1).broadcast_to([P, C2, CH]),
                                        ALU.mult).then_inc(M("dbu"), 1)

            def scan(q, n):
                step = NS * q + n
                e.wait_ge(M("dbu"), step + CRED + 1)
                e.wait_ge(M("dA"), 2 * step + 2)
                nc.vector.tensor_tensor_scan(state[n % AHEAD], dA[:, n % 2].rearrange("p h b t -> p (h b t)"),
                                             state[n % AHEAD], 0.0, ALU.mult, ALU.add).then_inc(M("scanned"), 1)

            def chunk(q, u, first, last, first_two=False):
                for n in range(NS):
                    if n < NS - 1:
                        times_b(q, n + 1)
                    elif not last:
                        times_b(q + 1, 0)
                    scan(q, n)
                    if n == 3 and not first:
                        y_out(q - 1, 1 - u)
                    if n == 9 and not first_two and not last:
                        dtu(q + 1)

            for q in range(NQ):
                dt(q)
                if q == NQ - 3:
                    times_b(0, 0)
            for u in range(2):
                chunk(u, u, u == 0, False, True)
            with e.Fori(1, NQ // 2 - 1) as r:
                for u in range(2):
                    chunk(2 * r + u, u, False, False)
            for u in range(2):
                chunk(NQ - 2 + u, u, False, u == 1)
            y_out(NQ - 1, 1)

        def mamba_residual(e, i):
            def add(g):
                e.wait_ge(M("o_psum"), g + 1)
                t = X[:, 4 * g:4 * g + 4, :].rearrange("p i d -> p (i d)")
                nc.vector.tensor_tensor(t, t, ps[:, g % 2, :], ALU.add).then_inc(M("x"), 1)

            if i % 4 == 0:
                if i == 0:
                    add(0)
                if i + 4 < NI:
                    add(i // 4 + 1)
                e.wait_ge(M("x"), i // 4 + 1)

        def mamba_pool(e):
            def lo(q, u, r):
                e.wait_ge(M("mid"), q + 1)
                nc.gpsimd.tensor_tensor(stack[64:96, bass.ds(CH * q, CH)], bcr[:, u, :],
                                        stack[32:64, bass.ds(CH * q, CH)], ALU.subtract).then_inc(M("stack"), 1)

            lo(0, 0, 0)
            pipeline(e, 2, NQ // 2, [(1, lo)])
            e.wait_ge(M("stack"), NQ + CRED)
            e.wait_ge(M("dt_psum"), NQ + CRED)
            nc.gpsimd.memset(dA[:, :, :, :, 0:1], 0.0).then_inc(M("dA_zero"), 1)
            e.wait_ge(M("dA_zero"), 1)
            for q in range(3):
                e.wait_ge(M("dt"), q + 1)
                nc.gpsimd.tensor_tensor(DTU[:, :, CH * q:CH * q + CH], DT[:, :, CH * q:CH * q + CH],
                                        HH[:, :, CH * q:CH * q + CH], ALU.mult).then_inc(M("dtu"), 1)
            with e.Fori(0, NQ) as q:
                for n in range(NS):
                    step = NS * q + n
                    e.wait_ge(M("scanned"), step + AHEAD + 1)
                    e.wait_ge(M("cs"), step + CRED + 1)
                    e.wait_ge(M("summed"), step - 2 + CRED + 1)
                    nc.gpsimd.tensor_tensor(prod[:, n % 2], state[n % AHEAD].rearrange("p (h t) -> p h t", h=C2),
                                            Cs[:, n % 2, :].unsqueeze(1).broadcast_to([P, C2, CH]),
                                            ALU.mult).then_inc(M("prod"), 1)

        block = ctx.enter_context(nc.Block())

        @block.sync
        def _(e):
            xv = x_in.rearrange("b (c i) d -> (b c) i d", i=NI)
            for q in range(4):
                e.dma_start(X[:, 8 * q:8 * q + 8, :], xv[:, 8 * q:8 * q + 8, :]).then_inc(G(f"x{q}"), 16)
            e.dma_start(gw[:, :], gate_w).then_inc(G("gw"), 16)
            e.dma_start(gb[:, :], gate_b.rearrange("(a n) -> a n", a=1)).then_inc(G("gb"), 16)
            e.dma_start(rows, b1).then_inc(G("rows"), 16)
            e.dma_start(b2_rows, b2).then_inc(G("b2"), 16)
            e.wait_ge(G("vrow0"), 1)
            e.dma_start(Win[:, :], W_in).then_inc(G("mw"), 16)
            e.dma_start(Wx[:, :, :], W_x.rearrange("(h p) n -> p h n", p=P)).then_inc(G("mw"), 16)
            e.dma_start(Wdt[:, :], W_dt).then_inc(G("mw"), 16)
            e.dma_start(Wout[:, :, :], W_out.rearrange("(h p) n -> p h n", p=P)).then_inc(G("mw"), 16)
            e.dma_start(An[:, :, :], A_log.rearrange("(h p) n -> p h n", p=P)).then_inc(G("mw"), 16)
            e.dma_start(vrow[0:KC, :], conv_w.rearrange("k o c -> k (o c)")).then_inc(G("mw"), 16)
            for k, v in enumerate((conv_b, b_dt, D_w)):
                e.dma_start(vrow[KC + k:KC + k + 1, :], v.rearrange("(a c) -> a c", a=1)).then_inc(G("mw"), 16)
            e.wait_ge(G("zeros"), 1)
            moe_sync(e, F[0], 0)
            for k in range(K):
                e.dma_start(y_dram[1][k * T:(k + 1) * T, :].rearrange("(p a i) d -> p a (i d)", p=P, a=8),
                            zeros[:, :].unsqueeze(1).broadcast_to([P, 8, 512])).then_inc(M("zeroed"), 16)
            e.wait_ge(M("o_psum"), 8)
            moe_sync(e, F[1], 1)
            for i0, i1 in OUT_PIECES:
                e.wait_ge(*F[1].at("x", i1 // 4))
                e.wait_ge(*F[1].at("x4", K * i1 // 4))
                e.dma_start(out.rearrange("b (c i) d -> (b c) i d", i=NI)[:, i0:i1, :],
                            X[:, i0:i1, :]).then_inc(G("out"), 16)
            e.wait_ge(G("out"), 16 * len(OUT_PIECES))

        @block.gpsimd
        def _(e):
            def expert_numbers():
                nc.gpsimd.iota(iotaE, pattern=[[1, E], [0, NI]], base=0, channel_multiplier=0,
                               allow_small_or_imprecise_dtypes=True).then_inc(G("code"), 1)

            nc.gpsimd.memset(vrow[:, :], 0.0).then_inc(G("vrow0"), 1)
            nc.gpsimd.memset(ident[:, :], 0.0).then_inc(G("id0"), 1)
            nc.gpsimd.memset(zeros[:, :], 0.0).then_inc(G("zeros"), 1)
            e.wait_ge(G("id0"), 1)
            nc.gpsimd.affine_select(out=ident[:, :], in_=ident[:, :], compare_op=ALU.not_equal, fill=1.0, base=0,
                                    pattern=[[-1, P]], channel_multiplier=1).then_inc(G("ident"), 1)
            expert_numbers()
            nc.gpsimd.iota(low[:, :, :], pattern=[[32, K], [1, NI]], base=0, channel_multiplier=0,
                           allow_small_or_imprecise_dtypes=True).then_inc(G("code"), 1)
            nc.gpsimd.iota(high[:, :], pattern=[[0, 1]], base=1, channel_multiplier=1,
                           allow_small_or_imprecise_dtypes=True).then_inc(G("code"), 1)
            nc.gpsimd.memset(earlier[:, :], 1.0).then_inc(G("ones"), 1)
            nc.gpsimd.memset(diag_m[:, :], -1.0).then_inc(G("ones"), 1)
            nc.gpsimd.memset(ones[:, :], 1.0).then_inc(G("ones"), 1)
            e.wait_ge(G("ones"), 3)
            nc.gpsimd.memset(one[:, :], 1.0).then_inc(G("one"), 1)
            e.wait_ge(G("one"), 1)
            nc.gpsimd.affine_select(out=earlier[:, :], in_=earlier[:, :], compare_op=ALU.is_gt, fill=0.0, base=0,
                                    pattern=[[1, P]], channel_multiplier=-1).then_inc(G("code"), 1)
            nc.gpsimd.affine_select(out=diag_m[:, :], in_=diag_m[:, :], compare_op=ALU.is_equal, fill=0.0, base=0,
                                    pattern=[[-1, P]], channel_multiplier=1).then_inc(G("code"), 1)
            nc.gpsimd.memset(sel[:, :], 0.0).then_inc(G("sel0"), 1)
            for name in ("sg", "h", "ts", "rest", "z", "dt_psum", "stack", "summed", "dbu",
                         "cs", "y"):
                e.sem_inc(M(name), CRED)
            e.sem_inc(M("conv"), 2 * CRED)
            e.sem_inc(M("scanned"), AHEAD)
            e.sem_inc(M("prod"), AHEAD)
            e.wait_ge(G("sel0"), 1)
            for g in range(3):
                e.wait_ge(G("sel"), g)
                part = sel[32 * g:32 * g + 32, :]
                nc.gpsimd.affine_select(out=part, in_=part, compare_op=ALU.not_equal, fill=1.0, base=0,
                                        pattern=[[-1, 2 * NS]], channel_multiplier=1)\
                    .then_inc(G("sel"), 1)
            e.wait_ge(G("sel"), 3)
            e.wait_ge(G("b2"), 16)
            nc.gpsimd.tensor_copy(b2_parts[:, 0, :], b2_rows).then_inc(G("b2_split"), 1)
            e.wait_ge(G("b2_split"), 1)
            nc.gpsimd.tensor_tensor(b2_rest, b2_rows, b2_parts[:, 0, :], ALU.subtract).then_inc(G("b2_split"), 1)
            e.wait_ge(G("b2_split"), 2)
            nc.gpsimd.tensor_copy(b2_parts[:, 1, :], b2_rest).then_inc(G("b2_split"), 1)
            e.wait_ge(G("b2_split"), 3)
            nc.gpsimd.tensor_tensor(b2_parts[:, 2, :], b2_rest, b2_parts[:, 1, :], ALU.subtract)\
                .then_inc(G("b2_split"), 1)
            e.wait_ge(G("b2_split"), 4)
            e.dma_start(b2_dram.rearrange("w e d -> e w d"), b2_parts).then_inc(G("b2_stored"), 16)
            moe_pool(e, F[0], LNS[0], 0)
            mamba_pool(e)
            e.wait_ge(M("o_psum"), 8)
            expert_numbers()
            moe_pool(e, F[1], LNS[2], 1)
            for s in range(RING):
                e.wait_ge(G(f"scattered{s}"), 2 * 16 * ROUNDS)

        @block.scalar
        def _(e):
            for c in range(HC):
                e.wait_ge(G("biasT"), c + 1)
                nc.scalar.activation(b1T[:, :].rearrange("p (j c a) -> p c a j", a=2, c=HC)[:, c],
                                     ps[:, 4 + c, 0:E].rearrange("p (a j) -> p a j", a=2), ACT.Copy)\
                    .then_inc(G("bias"), 1)
            e.wait_ge(G("mw"), 16 * 9)
            for h in range(C2):
                e.wait_ge(G("vT"), h + 1)
                nc.scalar.activation(vcol[:, h, :], ps[:, 2 + h, 0:8], ACT.Copy).then_inc(G("vcol"), 1)
            nc.scalar.activation(An[:, :, :], An[:, :, :], ACT.Exp).then_inc(G("A"), 1)
            e.wait_ge(G("A"), 1)
            nc.scalar.activation(An[:, :, :], An[:, :, :], ACT.Copy, scale=-1.0).then_inc(G("A"), 1)
            for h in range(C2):
                e.wait_ge(G("vcol"), h + 1)
                nc.scalar.activation(diagD[:, h, :], ident[:, :], ACT.Copy, scale=vcol[:, h, 6:7])\
                    .then_inc(M("diagD"), 1)
            moe_scalar(e, F[0], LNS[0], 0)
            e.wait_ge(G("A"), 2)
            mamba_scalar(e)
            moe_scalar(e, F[1], LNS[2], 1)

        @block.vector
        def _(e):
            moe_vector(e, F[0], LNS[0], 0, lambda i: e.wait_ge(G(f"x{i // 8}"), 16) if i % 8 == 0 else None)
            mamba_vector(e)
            moe_vector(e, F[1], LNS[2], 1, lambda i: mamba_residual(e, i))
            for g in range(8):
                moe_residual(e, F[1], 1, g)

        @block.tensor
        def _(e):
            e.wait_ge(G("ident"), 1)
            e.wait_ge(G("rows"), 16)
            for c in range(HC):
                nc.tensor.transpose(ps[:, 4 + c, 0:E], rows.rearrange("e (p c) -> e c p", c=HC)[:, c, :],
                                    ident[0:E, 0:E]).then_inc(G("biasT"), 1)
            e.wait_ge(G("mw"), 16 * 9)
            for h in range(C2):
                nc.tensor.transpose(ps[:, 2 + h, 0:8], vrow[:, h * P:(h + 1) * P], ident[0:8, 0:8])\
                    .then_inc(G("vT"), 1)
            e.wait_ge(G("vcol"), C2)
            e.wait_ge(G("bias"), HC)
            e.wait_ge(G("gw"), 16)
            e.wait_ge(G("gb"), 16)
            moe_tensor(e, F[0], LNS[0], 0)
            e.wait_ge(G("sel"), 3)
            mamba_tensor(e)
            moe_tensor(e, F[1], LNS[2], 1)


_INS = ['L0_attn_x', 'L0_attn_W_in', 'L0_attn_conv_w', 'L0_attn_conv_b', 'L0_attn_W_x', 'L0_attn_W_dt',
        'L0_attn_b_dt', 'L0_attn_A_log', 'L0_attn_D', 'L0_attn_W_out', 'L0_ffn_gate_w', 'L0_ffn_gate_b',
        'L0_ffn_w1', 'L0_ffn_b1', 'L0_ffn_w2', 'L0_ffn_b2']
_OUTS = [((BS, SEQ, D), 'float32')]


def kernel(**inputs):
    import numpy as _np
    import concourse.bacc as _bacc
    from concourse.bass_utils import run_bass_kernel_spmd as _run

    nc = _bacc.Bacc("TRN2", target_bir_lowering=False, num_devices=1)
    arrays, args = {}, []
    for name in _INS:
        a = _np.ascontiguousarray(inputs[name])
        arrays[f"in_{name}"] = a
        args.append(nc.dram_tensor(f"in_{name}", a.shape, mybir.dt.from_np(a.dtype), kind="ExternalInput").ap())
    for i, (shape, dtype) in enumerate(_OUTS):
        dt = mybir.dt.from_np(_np.dtype(dtype))
        args.append(nc.dram_tensor(f"out_{i}", shape, dt, kind="ExternalOutput").ap())
    macaron(nc, *args)
    r = _run(nc, [arrays], core_ids=[0])
    return r.results[0]["out_0"]
```
